# Optimizing a Trainium2 kernel written in Bass

```python
import numpy as np
import jax
import jax.numpy as jnp

def _softmax(x, axis=-1):
    return jax.nn.softmax(x, axis=axis)

def _gelu(x):
    return jax.nn.gelu(x, approximate=True)

def _silu(x):
    return jax.nn.silu(x)

def _sigmoid(x):
    return jax.nn.sigmoid(x)

def _layernorm(x, axis=-1, eps=1e-05):
    m = jnp.mean(x, axis=axis, keepdims=True)
    v = jnp.var(x, axis=axis, keepdims=True)
    return (x - m) / jnp.sqrt(v + eps)

def _scatter_add(tgt, idx, src, axis=0):
    return tgt.at[idx].add(src)

def _segment_sum(src, seg, n):
    return jax.ops.segment_sum(src, seg, n)
kernel_name = 'mk_recurrent_d2_jaxref_r8_d9c046'

def setup_inputs(seed: int=0):
    np.random.seed(seed)
    _w = jnp.asarray

    def _L0_attn_setup():
        import jax, jax.numpy as jnp
        import numpy as np
        EMBED_DIM = 128
        NUM_HEADS = 16
        D_K = EMBED_DIM // NUM_HEADS
        MAX_LEN = 128
        BATCH = 4
        SEQ = 128
        key = jax.random.key(seed)
        ks = jax.random.split(key, 6)
        s = 1.0 / np.sqrt(EMBED_DIM)
        return {'x': jax.random.normal(ks[0], (BATCH, SEQ, EMBED_DIM), jnp.float32), 'Wq': jax.random.normal(ks[1], (EMBED_DIM, EMBED_DIM), jnp.float32) * s, 'bq': jnp.zeros((EMBED_DIM,), jnp.float32), 'Wk': jax.random.normal(ks[2], (EMBED_DIM, EMBED_DIM), jnp.float32) * s, 'bk': jnp.zeros((EMBED_DIM,), jnp.float32), 'Wv': jax.random.normal(ks[3], (EMBED_DIM, EMBED_DIM), jnp.float32) * s, 'bv': jnp.zeros((EMBED_DIM,), jnp.float32), 'Wo': jax.random.normal(ks[4], (EMBED_DIM, EMBED_DIM), jnp.float32) * s, 'bo': jnp.zeros((EMBED_DIM,), jnp.float32), 'rel_table': jax.random.normal(ks[5], (2 * MAX_LEN - 1, D_K), jnp.float32)}
    _L0_attn_in = _L0_attn_setup()

    def _L0_ffn_setup():
        import jax, jax.numpy as jnp
        import numpy as np
        NUM_EXPERTS = 8
        D_MODEL = 128
        D_OUT = 128
        key = jax.random.key(seed)
        ks = jax.random.split(key, 5)
        B, S = (2, 256)
        x = jax.random.normal(ks[0], (B, S, D_MODEL), dtype=jnp.float32)
        gate_w = jax.random.normal(ks[1], (D_MODEL, NUM_EXPERTS), dtype=jnp.float32) * 0.02
        gate_b = jnp.zeros((NUM_EXPERTS,), dtype=jnp.float32)
        expert_w = jax.random.normal(ks[2], (NUM_EXPERTS, D_MODEL, D_OUT), dtype=jnp.float32) * 0.02
        expert_b = jnp.zeros((NUM_EXPERTS, D_OUT), dtype=jnp.float32)
        return {'x': x, 'gate_w': gate_w, 'gate_b': gate_b, 'expert_w': expert_w, 'expert_b': expert_b}
    _L0_ffn_in = _L0_ffn_setup()

    def _L1_attn_setup():
        import jax, jax.numpy as jnp
        import numpy as np
        import math
        DIM = 128
        NUM_HEADS = 8
        HEAD_DIM = DIM // NUM_HEADS // 2
        DEPTH = 6
        LAMBDA_INIT = 0.8 - 0.6 * math.exp(-0.3 * DEPTH)
        EPS = 1e-05
        key = jax.random.key(seed)
        ks = jax.random.split(key, 10)
        B, S = (2, 256)
        x = jax.random.normal(ks[0], (B, S, DIM), dtype=jnp.float32)
        sc = DIM ** (-0.5)
        Wq = jax.random.normal(ks[1], (DIM, DIM), dtype=jnp.float32) * sc
        Wk = jax.random.normal(ks[2], (DIM, DIM), dtype=jnp.float32) * sc
        Wv = jax.random.normal(ks[3], (DIM, DIM), dtype=jnp.float32) * sc
        Wo = jax.random.normal(ks[4], (DIM, DIM), dtype=jnp.float32) * sc
        lq1 = jax.random.normal(ks[5], (HEAD_DIM,), dtype=jnp.float32) * 0.1
        lk1 = jax.random.normal(ks[6], (HEAD_DIM,), dtype=jnp.float32) * 0.1
        lq2 = jax.random.normal(ks[7], (HEAD_DIM,), dtype=jnp.float32) * 0.1
        lk2 = jax.random.normal(ks[8], (HEAD_DIM,), dtype=jnp.float32) * 0.1
        return {'x': x, 'Wq': Wq, 'Wk': Wk, 'Wv': Wv, 'Wo': Wo, 'lq1': lq1, 'lk1': lk1, 'lq2': lq2, 'lk2': lk2}
    _L1_attn_in = _L1_attn_setup()

    def _L1_ffn_setup():
        import jax, jax.numpy as jnp
        import numpy as np
        S, B, H, F, E, K = (256, 2, 128, 256, 8, 2)

        def _moe_forward(hidden_states, router_w, w1, b1, w2, b2):
            s, b, h = hidden_states.shape
            T = s * b
            x = hidden_states.reshape(T, h)
            logits = jnp.einsum('th,eh->te', x, router_w)
            topk_logits, topk_idx = jax.lax.top_k(logits, K)
            probs = jax.nn.softmax(topk_logits, axis=-1)
            combine = jnp.zeros((T, E), dtype=x.dtype)
            combine = combine.at[jnp.arange(T)[:, None], topk_idx].add(probs.astype(x.dtype))
            hmid = jnp.einsum('th,efh->etf', x, w1) + b1[:, None, :]
            hmid = jax.nn.gelu(hmid, approximate=False)
            y = jnp.einsum('etf,ehf->eth', hmid, w2) + b2[:, None, :]
            out = jnp.einsum('eth,te->th', y, combine)
            return out.reshape(s, b, h)
        key = jax.random.key(seed)
        ks = jax.random.split(key, 6)
        std = 0.02
        return {'hidden_states': jax.random.normal(ks[0], (S, B, H), dtype=jnp.float32), 'router_w': jax.random.normal(ks[1], (E, H), dtype=jnp.float32) * std, 'w1': jax.random.normal(ks[2], (E, F, H), dtype=jnp.float32) * (1.0 / np.sqrt(H)), 'b1': jnp.zeros((E, F), dtype=jnp.float32), 'w2': jax.random.normal(ks[3], (E, H, F), dtype=jnp.float32) * (1.0 / np.sqrt(F)), 'b2': jnp.zeros((E, H), dtype=jnp.float32)}
    _L1_ffn_in = _L1_ffn_setup()
    _d = {'L0_attn_x': _L0_attn_in['x'], 'L0_attn_Wq': _L0_attn_in['Wq'], 'L0_attn_bq': _L0_attn_in['bq'], 'L0_attn_Wk': _L0_attn_in['Wk'], 'L0_attn_bk': _L0_attn_in['bk'], 'L0_attn_Wv': _L0_attn_in['Wv'], 'L0_attn_bv': _L0_attn_in['bv'], 'L0_attn_Wo': _L0_attn_in['Wo'], 'L0_attn_bo': _L0_attn_in['bo'], 'L0_attn_rel_table': _L0_attn_in['rel_table'], 'L0_ffn_gate_w': _L0_ffn_in['gate_w'], 'L0_ffn_gate_b': _L0_ffn_in['gate_b'], 'L0_ffn_expert_w': _L0_ffn_in['expert_w'], 'L0_ffn_expert_b': _L0_ffn_in['expert_b'], 'L1_attn_Wq': _L1_attn_in['Wq'], 'L1_attn_Wk': _L1_attn_in['Wk'], 'L1_attn_Wv': _L1_attn_in['Wv'], 'L1_attn_Wo': _L1_attn_in['Wo'], 'L1_attn_lq1': _L1_attn_in['lq1'], 'L1_attn_lk1': _L1_attn_in['lk1'], 'L1_attn_lq2': _L1_attn_in['lq2'], 'L1_attn_lk2': _L1_attn_in['lk2'], 'L1_ffn_router_w': _L1_ffn_in['router_w'], 'L1_ffn_w1': _L1_ffn_in['w1'], 'L1_ffn_b1': _L1_ffn_in['b1'], 'L1_ffn_w2': _L1_ffn_in['w2'], 'L1_ffn_b2': _L1_ffn_in['b2']}
    _x0 = _d['L0_attn_x']
    _d['L0_attn_x'] = jax.random.normal(jax.random.fold_in(jax.random.key(seed), 1), (4, 1024, 128), dtype=_x0.dtype)
    del _x0
    return _d

def reference(L0_attn_x, L0_attn_Wq, L0_attn_bq, L0_attn_Wk, L0_attn_bk, L0_attn_Wv, L0_attn_bv, L0_attn_Wo, L0_attn_bo, L0_attn_rel_table, L0_ffn_gate_w, L0_ffn_gate_b, L0_ffn_expert_w, L0_ffn_expert_b, L1_attn_Wq, L1_attn_Wk, L1_attn_Wv, L1_attn_Wo, L1_attn_lq1, L1_attn_lk1, L1_attn_lq2, L1_attn_lk2, L1_ffn_router_w, L1_ffn_w1, L1_ffn_b1, L1_ffn_w2, L1_ffn_b2):

    def _L0_attn_ref(x, Wq, bq, Wk, bk, Wv, bv, Wo, bo, rel_table):
        import jax, jax.numpy as jnp
        import numpy as np
        EMBED_DIM = 128
        NUM_HEADS = 16
        D_K = EMBED_DIM // NUM_HEADS
        MAX_LEN = 128
        BATCH = 4
        SEQ = 128
        b, n, e = x.shape
        h, d = (NUM_HEADS, D_K)

        def proj(W, bias):
            y = jnp.einsum('bne,fe->bnf', x, W) + bias
            return y.reshape(b, n, h, d).transpose(0, 2, 1, 3)
        Q = proj(Wq, bq)
        K = proj(Wk, bk)
        V = proj(Wv, bv)
        scores_content = jnp.einsum('bhid,bhjd->bhij', Q, K)
        pos = jnp.arange(n)
        rel_pos = jnp.clip(pos[:, None] - pos[None, :] + MAX_LEN - 1, 0, 2 * MAX_LEN - 2)
        rel_emb = rel_table[rel_pos]
        scores_pos = jnp.einsum('bhid,ijd->bhij', Q, rel_emb)
        scores = (scores_content + scores_pos) / np.sqrt(d).astype(np.float32)
        attn = jax.nn.softmax(scores, axis=-1)
        out = jnp.einsum('bhij,bhjd->bhid', attn, V)
        out = out.transpose(0, 2, 1, 3).reshape(b, n, e)
        return jnp.einsum('bne,fe->bnf', out, Wo) + bo

    def _L0_ffn_ref(x, gate_w, gate_b, expert_w, expert_b):
        import jax, jax.numpy as jnp
        import numpy as np
        NUM_EXPERTS = 8
        D_MODEL = 128
        D_OUT = 128
        orig_shape = x.shape
        xt = x.reshape(-1, D_MODEL)
        logits = xt @ gate_w + gate_b
        gates = jax.nn.softmax(logits, axis=-1)
        sel = jnp.argmax(gates, axis=-1)
        onehot = jax.nn.one_hot(sel, NUM_EXPERTS, dtype=xt.dtype)
        y_all = jnp.einsum('td,edh->eth', xt, expert_w) + expert_b[:, None, :]
        out = jnp.einsum('te,eth->th', onehot, y_all)
        return out.reshape(*orig_shape[:-1], D_OUT)

    def _L1_attn_ref(x, Wq, Wk, Wv, Wo, lq1, lk1, lq2, lk2):
        import jax, jax.numpy as jnp
        import numpy as np
        import math
        DIM = 128
        NUM_HEADS = 8
        HEAD_DIM = DIM // NUM_HEADS // 2
        DEPTH = 6
        LAMBDA_INIT = 0.8 - 0.6 * math.exp(-0.3 * DEPTH)
        EPS = 1e-05
        B, S, D = x.shape
        H, hd = (NUM_HEADS, HEAD_DIM)
        scaling = hd ** (-0.5)
        q = (x @ Wq.T).reshape(B, S, 2 * H, hd).transpose(0, 2, 1, 3) * scaling
        k = (x @ Wk.T).reshape(B, S, 2 * H, hd).transpose(0, 2, 1, 3)
        v = (x @ Wv.T).reshape(B, S, H, 2 * hd).transpose(0, 2, 1, 3)
        scores = jnp.einsum('bhqd,bhkd->bhqk', q, k)
        scores = jnp.nan_to_num(scores)
        causal = jnp.triu(jnp.full((S, S), -jnp.inf, dtype=scores.dtype), 1)
        attn = jax.nn.softmax(scores + causal, axis=-1)
        lam1 = jnp.exp(jnp.sum(lq1 * lk1))
        lam2 = jnp.exp(jnp.sum(lq2 * lk2))
        lam = lam1 - lam2 + LAMBDA_INIT
        attn = attn.reshape(B, H, 2, S, S)
        w = attn[:, :, 0] - lam * attn[:, :, 1]
        o = jnp.einsum('bhqk,bhkd->bhqd', w, v)
        o = o * jax.lax.rsqrt(jnp.mean(o * o, axis=-1, keepdims=True) + EPS)
        o = o * (1.0 - LAMBDA_INIT)
        o = o.transpose(0, 2, 1, 3).reshape(B, S, H * 2 * hd)
        return o @ Wo.T

    def _L1_ffn_ref(hidden_states, router_w, w1, b1, w2, b2):
        import jax, jax.numpy as jnp
        import numpy as np
        S, B, H, F, E, K = (256, 2, 128, 256, 8, 2)

        def _moe_forward(hidden_states, router_w, w1, b1, w2, b2):
            s, b, h = hidden_states.shape
            T = s * b
            x = hidden_states.reshape(T, h)
            logits = jnp.einsum('th,eh->te', x, router_w)
            topk_logits, topk_idx = jax.lax.top_k(logits, K)
            probs = jax.nn.softmax(topk_logits, axis=-1)
            combine = jnp.zeros((T, E), dtype=x.dtype)
            combine = combine.at[jnp.arange(T)[:, None], topk_idx].add(probs.astype(x.dtype))
            hmid = jnp.einsum('th,efh->etf', x, w1) + b1[:, None, :]
            hmid = jax.nn.gelu(hmid, approximate=False)
            y = jnp.einsum('etf,ehf->eth', hmid, w2) + b2[:, None, :]
            out = jnp.einsum('eth,te->th', y, combine)
            return out.reshape(s, b, h)
        return _moe_forward(hidden_states, router_w, w1, b1, w2, b2)
    x = L0_attn_x
    xn = _layernorm(x, axis=-1)
    s = _L0_attn_ref(xn, L0_attn_Wq, L0_attn_bq, L0_attn_Wk, L0_attn_bk, L0_attn_Wv, L0_attn_bv, L0_attn_Wo, L0_attn_bo, L0_attn_rel_table)
    g = _silu(_L0_ffn_ref(xn, L0_ffn_gate_w, L0_ffn_gate_b, L0_ffn_expert_w, L0_ffn_expert_b))
    x = x + s * g
    xn = _layernorm(x, axis=-1)
    s = _L1_attn_ref(xn, L1_attn_Wq, L1_attn_Wk, L1_attn_Wv, L1_attn_Wo, L1_attn_lq1, L1_attn_lk1, L1_attn_lq2, L1_attn_lk2)
    g = _silu(_L1_ffn_ref(xn, L1_ffn_router_w, L1_ffn_w1, L1_ffn_b1, L1_ffn_w2, L1_ffn_b2))
    x = x + s * g
    return x

_drawn_inputs = setup_inputs


def setup_inputs(seed=0):
    import zlib

    import numpy as np

    out = dict(_drawn_inputs(seed))
    spreads = {'L0_attn_bq': (0.0, 0.8),
     'L0_attn_bk': (0.0, 0.8),
     'L0_attn_bv': (0.0, 0.537),
     'L0_attn_bo': (0.0, 0.512),
     'L0_ffn_gate_b': (0.0, 0.351),
     'L0_ffn_expert_b': (0.0, 0.68),
     'L1_ffn_b1': (0.0, 0.8),
     'L1_ffn_b2': (0.0, 0.681)}
    factors = {'L0_attn_Wq': 3.327,
     'L0_attn_Wk': 3.357,
     'L0_attn_Wv': 3.142,
     'L0_attn_rel_table': 5.084,
     'L1_attn_lq1': 8.0,
     'L1_attn_lk1': 8.0,
     'L1_attn_lq2': 8.0,
     'L1_attn_lk2': 8.0}
    for name, (base, spread) in spreads.items():
        noise = np.random.default_rng([zlib.crc32(name.encode()), seed]).standard_normal(out[name].shape)
        drawn = base * np.exp(spread * noise) if base else spread * noise
        out[name] = jnp.asarray(drawn.astype(out[name].dtype))
    for name, factor in factors.items():
        out[name] = (out[name] * factor).astype(out[name].dtype)
    return out
```

```python
import concourse.bass as bass
from concourse import mybir
from contextlib import ExitStack
import numpy as np

F32 = mybir.dt.float32
BF16 = mybir.dt.bfloat16
ALU = mybir.AluOpType
ACT = mybir.ActivationFunctionType
AX = mybir.AxisListType

P = 128
B, S, D = 4, 1024, 128
T = B * S
GROUP = 512
GT = GROUP // P
GROUPS = T // GROUP
H = 16
DH = 8
PAIRS = H // 2
NB = S // P
SLOTS = 6
QPART = [0, 0, 0, 1, 1, 2]
KPART = [0, 1, 2, 0, 1, 0]
ROWS = SLOTS * DH
KD = 2 * ROWS
KM = KD + 3
MAXLEN = 128
CH = 4
HALF = P // 2
CQ = HALF // CH
Y0 = P + HALF - 1
YW = Y0 + 2 * P
E = 8
FF = 256
LAMBDA_INIT = 0.8 - 0.6 * float(np.exp(-0.3 * 6))
EPS = 1e-5
SCALE = float(DH) ** -0.5
BIG = 1e30
CLAMP = 1e18
ER = 4
QR = 3


def position_table_rows(rel):
    y = np.arange(YW)
    out = [rel[np.clip(HALF * a + MAXLEN - 1 - (y - Y0), 0, 2 * MAXLEN - 2)].T for a in range(2) for _ in range(SLOTS)]
    return np.concatenate(out, 0)


def attention_plan(layer):
    plan = []
    nmax = nexp = njb = 0
    for s in range(NB + 2):
        items = []
        if s < NB:
            ib, m = s, []
            if layer == 0:
                for jb in range(NB):
                    for c in range(CH):
                        m.append(("max", ib, jb, c))
                for c in range(4):
                    m.append(("maxt", ib, None, c))
            else:
                for h in range(H):
                    for half in range(1 + ib // 4):
                        m.append(("max", ib, half, h))
            for k, it in enumerate(m):
                items.append(((k + 0.5) / len(m) * 0.78, it + (nmax,)))
                nmax += 1
            items.append((0.84, ("mrow", ib)))
            items.append((0.86, ("msplit", ib)))
        if 1 <= s <= NB:
            ib, m = s - 1, []
            jbs = range(NB if layer == 0 else ib + 1)
            for jb in jbs:
                for half in range(2):
                    m.append(("exp", ib, jb, half, nexp, njb + jb))
                    nexp += 1
                if jb:
                    m.append(("av", ib, jb - 1, njb + jb - 1, len(jbs)))
            m.append(("av", ib, len(jbs) - 1, njb + len(jbs) - 1, len(jbs)))
            njb += len(jbs)
            for k, it in enumerate(m):
                items.append(((k + 0.5) / len(m), it))
        if s >= 2:
            ib = s - 2
            last = sum(NB if layer == 0 else i + 1 for i in range(ib + 1)) - 1
            for at, kind in ((0.06, "ocopy"), (0.12, "oback"), (0.2, "onorm"), (0.3, "oturn"), (0.4, "oturned"),
                             (0.5, "oproj"), (0.6, "final")):
                items.append((at, (kind, ib, last)))
            if layer == 1:
                items += [(0.23, ("orms", ib)), (0.26, ("oscale", ib))]
        items.sort(key=lambda x: x[0])
        plan += [it for _, it in items]
    return plan, nmax, nexp, njb


def build(nc, ins, out):
    ctx = ExitStack()
    with ctx:
        def sb(name, shape, dt=F32):
            return ctx.enter_context(nc.sbuf_tensor(name, shape, dt))

        def sem(name):
            return ctx.enter_context(nc.semaphore(name))

        def dram(name, shape, dt=F32):
            return nc.dram_tensor(name, shape, dt, kind="Internal").ap()

        bank = ctx.enter_context(nc.psum_tensor("bank", [P, 8, 512], F32))

        eye = sb("eye", [P, P])
        eye_b = sb("eye_b", [P, P], BF16)
        mask_f = sb("mask_f", [P, 2, P])
        mask_b = sb("mask_b", [P, 2, P], BF16)
        rank = sb("rank", [P, GT, E])
        levels = sb("levels", [KD, 2])
        rel_f = sb("rel_f", [KD, YW])
        rel_r = sb("rel_r", [KD, YW])
        rel_p = sb("rel_p", [KD, YW], BF16)
        rel_p2 = sb("rel_p2", [KD, YW], BF16)
        rel_t = sb("rel_t", [KD, YW], BF16)
        col = sb("col", [P, 5])
        bk2 = sb("bk2", [P, 2])
        bv = sb("bv", [P, D])
        bo = sb("bo", [1, D])
        ones_row = sb("ones_row", [1, P])
        gate_b = sb("gate_b", [P, E])
        lam_in = sb("lam_in", [P, 4, DH])
        lam_w = sb("lam_w", [P, 2, DH])
        lam_s = sb("lam_s", [P, 4])
        w = {}
        for n in ("q", "k", "v", "o"):
            for layer in range(2):
                w[n, layer] = sb(f"w{n}{layer}", [P, P])
        gate_w = [sb("gate_w0", [P, E]), sb("gate_w1", [P, E])]
        exp_w = sb("exp_w", [P, E, P])
        out_b = [sb("out_b0", [E, P]), sb("out_b1", [E, P])]
        w1 = sb("w1", [P, E, FF])
        b1 = sb("b1", [P, E, 2])
        w2 = sb("w2", [P, E, 2, P])

        X = sb("X", [P, GT, P])
        stats = sb("stats", [P, GT, 6])
        mv = sb("mv", [P, GT, 2])
        rstd = sb("rstd", [P, GT])
        XN = sb("XN", [P, GT, P])
        XT = sb("XT", [P, GROUP])
        FQ = sb("FQ", [P, 3, GROUP])
        FR = sb("FR", [P, 3, GROUP])
        PARTS = sb("PARTS", [P, 3, 3, GROUP], BF16)
        VA = [sb("VA0", [P, GT, H, DH + 1]), sb("VA1", [P, GT, PAIRS, 2 * DH + 1])]
        LG = sb("LG", [P, GT, E])
        L2 = sb("L2", [P, GT, E])
        SEL = sb("SEL", [P, GT, E])
        OH = sb("OH", [P, 2, GT, E])
        MX = sb("MX", [P, 4, GT])
        C = sb("C", [P, GT, E])
        CT = sb("CT", [E, GROUP])
        HM = sb("HM", [P, 2, 2, GROUP])
        ACC = sb("ACC", [P, GT, P])
        G = sb("G", [P, GT, P])

        KS = sb("KS", [P, 2, PAIRS, S], BF16)
        QS = sb("QS", [P, QR, PAIRS, 2, P], BF16)
        QP = sb("QP", [KD, QR, H, P], BF16)
        VV = sb("VV", [P, NB, 168])
        EX = sb("EX", [P, ER, H * P])
        PM = sb("PM", [P, 2, H, P])
        M2 = sb("M2", [P, H, 2])
        M = sb("M", [P, H])
        MP = sb("MP", [H, 2, 3, P], BF16)
        MR = sb("MR", [H, P])
        OS = sb("OS", [P, 512])
        RC = sb("RC", [P, H])
        ON = sb("ON", [P, H, 2 * DH])
        OD = sb("OD", [P, PAIRS, 2 * DH])
        OQ = sb("OQ", [P, PAIRS, 2 * DH])
        SS = sb("SS", [P, PAIRS])
        OF = sb("OF", [P, P])
        OT = sb("OT", [P, P])
        XG = sb("XG", [P, 2, 2, P])
        TM = sb("TM", [P, P])
        XO = sb("XO", [P, 2, P])

        x_mid = dram("x_mid", (T, D))
        g_dram = dram("g_dram", (T, D))
        q_dram = dram("q_dram", (B, H, ROWS, S), BF16)
        k_dram = dram("k_dram", (2, B, H, ROWS, S), BF16)
        v_dram = [dram("v_dram0", (T, H * (DH + 1))), dram("v_dram1", (T, PAIRS * (2 * DH + 1)))]

        weights_in = sem("weights_in")
        waited = sem("waited")
        setup_done = sem("setup_done")
        lam_exp = sem("lam_exp")
        lam_sum = sem("lam_sum")

        loads = [
            (eye[:, :], ins["eye"]), (mask_f[:, :, :], ins["mask"]), (rank[:, :, :], ins["rank"]),
            (levels[:, :], ins["levels"]), (rel_f[:, :], ins["rel"]), (col[:, 0:4], ins["cols"]),
            (bv[:, :], ins["bv"]), (bo[:, :], ins["bo"]), (gate_b[:, :], ins["gate_b"]),
            (lam_in[:, :, :], ins["lam"]), (gate_w[0][:, :], ins["gate_w"]), (gate_w[1][:, :], ins["router_w"]),
            (exp_w[:, :, :], ins["expert_w"]), (out_b[0][:, :], ins["expert_b"]), (out_b[1][:, :], ins["b2"]),
            (w1[:, :, :], ins["w1"]), (b1[:, :, :], ins["b1"]), (w2[:, :, :, :], ins["w2"]),
        ] + [(w[n, layer][:, :], ins[f"W{n}{layer}"]) for n in "qkvo" for layer in range(2)]
        LOADED = 16 * len(loads)

        with nc.Block() as block:
            @block.sync
            def _(sp):
                for dst, src in loads:
                    sp.dma_start(dst, src).then_inc(weights_in, 16)

            @block.gpsimd
            def _(pool):
                pool.memset(QS[:, :, :, :, :], 0.0)
                pool.memset(QP[:, :, :, :], 0.0)
                pool.memset(KS[:, :, :, :], 1.0)
                pool.memset(ones_row[:, :], 1.0)
                pool.memset(VA[0][:, :, :, :], 1.0)
                pool.memset(VA[1][:, :, :, :], 1.0)
                pool.memset(VV[:, :, :], 0.0).then_inc(setup_done, 1)
                pool.drain()

            @block.vector
            def _(dve):
                dve.wait_ge(weights_in, LOADED)
                dve.tensor_copy(eye_b[:, :], eye[:, :])
                dve.tensor_copy(mask_b[:, :, :], mask_f[:, :, :])
                dve.tensor_scalar(bk2[:, 0:1], col[:, 1:2], col[:, 2:3], None, ALU.add)
                dve.tensor_scalar(bk2[:, 1:2], col[:, 1:2], col[:, 3:4], None, ALU.add)
                dve.tensor_scalar(rel_r[:, :], rel_f[:, :], rel_f[:, 0:1], None, ALU.subtract)
                dve.drain()
                dve.tensor_copy(rel_p[:, :], rel_r[:, :])
                dve.drain()
                dve.scalar_tensor_tensor(rel_f[:, :], rel_p[:, :], levels[:, 0:1], rel_r[:, :], ALU.mult, ALU.add)
                dve.drain()
                dve.tensor_copy(rel_p2[:, :], rel_f[:, :])
                dve.drain()
                dve.scalar_tensor_tensor(rel_t[:, :], rel_p2[:, :], levels[:, 1:2], rel_f[:, :], ALU.mult, ALU.add)
                dve.tensor_tensor(lam_w[:, :, :], lam_in[:, 0:2, :], lam_in[:, 2:4, :], ALU.mult)
                dve.drain()
                dve.tensor_reduce(lam_s[:, 0:2], lam_w[:, :, :], AX.X, ALU.add).then_inc(lam_sum, 1)
                dve.wait_ge(lam_exp, 1)
                dve.tensor_tensor(lam_s[:, 2:3], lam_s[:, 1:2], lam_s[:, 0:1], ALU.subtract)
                dve.drain()
                dve.tensor_scalar(lam_s[:, 3:4], lam_s[:, 2:3], -LAMBDA_INIT, None, ALU.add).then_inc(setup_done, 1)

            @block.scalar
            def _(act):
                act.wait_ge(lam_sum, 1)
                act.activation(lam_s[:, 0:2], lam_s[:, 0:2], ACT.Exp).then_inc(lam_exp, 1)

        neg_lam = lam_s[:, 3:4]

        def token_stage(layer, x_src):
            n = f"t{layer}_"
            streams = 3 if layer == 0 else 2
            x_in, x_free = sem(n + "x_in"), sem(n + "x_free")
            var_ready, ln_ready, rstd_ready = sem(n + "var_ready"), sem(n + "ln_ready"), sem(n + "rstd_ready")
            xn_ready, xt_psum, xt_ready = sem(n + "xn_ready"), sem(n + "xt_psum"), sem(n + "xt_ready")
            proj_psum, proj_used = sem(n + "proj_psum"), sem(n + "proj_used")
            f_ready, p1_ready, r_ready, p2_ready = (sem(n + s) for s in ("f_ready", "p1_ready", "r_ready", "p2_ready"))
            parts_ready, v_ready, qk_stored, v_stored = (sem(n + s) for s in ("parts_ready", "v_ready", "qk_stored", "v_stored"))
            logits_psum, c_ready, ct_psum, ct_ready, bias_psum = (
                sem(n + s) for s in ("logits_psum", "c_ready", "ct_psum", "ct_ready", "bias_psum"))
            diff_ready, odds_ready = sem(n + "diff_ready"), sem(n + "odds_ready")
            hid_psum, hid_ready = sem(n + "hid_psum"), sem(n + "hid_ready")
            y_psum, y_used = sem(n + "y_psum"), sem(n + "y_used")
            acc_ready, g_ready, g_stored = sem(n + "acc_ready"), sem(n + "g_ready"), sem(n + "g_stored")
            QKDMA = 16 * SLOTS * streams
            vw = VA[layer]
            x_v = x_src.rearrange("(g t p) d -> g p t d", t=GT, p=P)
            g_v = g_dram.rearrange("(g t p) d -> g p t d", t=GT, p=P)
            v_v = v_dram[layer].rearrange("(g t p) d -> g p t d", t=GT, p=P)
            halves = S // GROUP

            with nc.Block() as block:
                @block.gpsimd
                def _(pool):
                    with pool.Fori(0, GROUPS) as g:
                        pool.wait_ge(x_free, g + 1)
                        pool.sem_inc(waited, 1)
                        pool.dma_start(X[:, :, :], x_v[g]).then_inc(x_in, 16)

                @block.sync
                def _(sp):
                    with sp.Fori(0, B) as b:
                        for c in range(halves):
                            g = b * halves + c
                            span = slice(c * GROUP, (c + 1) * GROUP)
                            sp.wait_ge(v_ready, g + 1)
                            sp.dma_start(v_v[g], vw[:, :, :, :].rearrange("p t h d -> p t (h d)")).then_inc(v_stored, 16)
                            sp.wait_ge(parts_ready, g + 1)
                            for s in range(SLOTS):
                                row = slice(s * DH, (s + 1) * DH)
                                sp.dma_start(q_dram[b][:, row, span], PARTS[:, QPART[s], 0, :]).then_inc(qk_stored, 16)
                                for v in range(streams - 1):
                                    sp.dma_start(k_dram[v][b][:, row, span], PARTS[:, KPART[s], 1 + v, :])\
                                      .then_inc(qk_stored, 16)
                            sp.wait_ge(g_ready, g + 2)
                            sp.dma_start(g_v[g], G[:, :, :]).then_inc(g_stored, 16)
                    sp.wait_ge(v_stored, 16 * GROUPS + 1)
                    sp.wait_ge(qk_stored, QKDMA * GROUPS + 1)
                    sp.wait_ge(g_stored, 16 * GROUPS + 1)

                @block.scalar
                def _(act):
                    if layer == 0:
                        act.wait_ge(setup_done, 2)
                    with act.Fori(0, GROUPS) as g:
                        act.wait_ge(var_ready, g + 1)
                        act.activation(rstd[:, :], rstd[:, :], ACT.Ln).then_inc(ln_ready, 1)
                        act.wait_ge(ln_ready, g + 1)
                        act.activation(rstd[:, :], rstd[:, :], ACT.Exp, scale=-0.5).then_inc(rstd_ready, 1)
                        act.wait_ge(xt_psum, g + 1)
                        act.activation(XT[:, :], bank[:, 0, :], ACT.Copy).then_inc(xt_ready, 1)
                        act.wait_ge(qk_stored, g * QKDMA + 1)
                        act.wait_ge(f_ready, g + 1)
                        act.activation(PARTS[:, 0, 0:streams, :], FQ[:, 0:streams, :], ACT.Copy).then_inc(p1_ready, 1)
                        act.wait_ge(r_ready, g + 1)
                        act.activation(PARTS[:, 1, 0:streams, :], FR[:, 0:streams, :], ACT.Copy).then_inc(p2_ready, 1)
                        if layer == 1:
                            act.wait_ge(diff_ready, g + 1)
                            act.activation(MX[:, 3, :], MX[:, 2, :], ACT.Exp).then_inc(odds_ready, 1)
                        act.wait_ge(ct_psum, g + 1)
                        act.activation(CT[:, :], bank[0:E, 4, :], ACT.Copy).then_inc(ct_ready, 1)
                        if layer == 1:
                            for e in range(E):
                                for f in range(2):
                                    act.wait_ge(hid_psum, g * 2 * E + 2 * e + f + 1)
                                    act.activation(HM[:, e % 2, f, :], bank[:, 1 + f, :], ACT.Gelu,
                                                   bias=b1[:, e, f:f + 1]).then_inc(hid_ready, 1)
                        act.wait_ge(acc_ready, g + 1)
                        act.wait_ge(g_stored, g * 16 + 1)
                        act.activation(G[:, :, :], ACC[:, :, :], ACT.Silu).then_inc(g_ready, 1)

                @block.tensor
                def _(pe):
                    if layer == 0:
                        pe.wait_ge(weights_in, LOADED)
                        pe.wait_ge(setup_done, 2)
                    with pe.Fori(0, GROUPS) as g:
                        pe.wait_ge(xn_ready, g + 1)
                        for t in range(GT):
                            last = pe.transpose(bank[:, 0, t * P:(t + 1) * P], XN[:, t, :], eye[:, :])
                        last.then_inc(xt_psum, 1)
                        pe.wait_ge(xt_ready, g + 1)
                        pe.wait_ge(proj_used, 3 * g + 3)
                        pe.matmul(bank[:, 1, :], w["q", layer][:, :], XT[:, :], start=True, stop=True).then_inc(proj_psum, 1)
                        pe.matmul(bank[:, 2, :], w["k", layer][:, :], XT[:, :], start=True, stop=True).then_inc(proj_psum, 1)
                        for t in range(GT):
                            last = pe.matmul(bank[:, 3, t * P:(t + 1) * P], XT[:, t * P:(t + 1) * P],
                                             w["v", layer][:, :], start=True, stop=True)
                        last.then_inc(proj_psum, 1)
                        for t in range(GT):
                            last = pe.matmul(bank[:, 4, t * E:(t + 1) * E], XT[:, t * P:(t + 1) * P],
                                             gate_w[layer][:, :], start=True, stop=True)
                        last.then_inc(logits_psum, 1)
                        pe.wait_ge(c_ready, g + 1)
                        for t in range(GT):
                            last = pe.transpose(bank[0:E, 4, t * P:(t + 1) * P], C[:, t, :], eye[:, :])
                        last.then_inc(ct_psum, 1)
                        pe.wait_ge(ct_ready, g + 1)
                        for t in range(GT):
                            last = pe.matmul(bank[:, 5, t * P:(t + 1) * P], CT[:, t * P:(t + 1) * P],
                                             out_b[layer][:, :], start=True, stop=True)
                        last.then_inc(bias_psum, 1)

                        def y_bank(e):
                            pe.wait_ge(y_used, g * E + e + 1)

                        if layer == 0:
                            for e in range(E):
                                y_bank(e)
                                for t in range(GT):
                                    last = pe.matmul(bank[:, 6 + e % 2, t * P:(t + 1) * P], XT[:, t * P:(t + 1) * P],
                                                     exp_w[:, e, :], start=True, stop=True)
                                last.then_inc(y_psum, 1)
                        else:
                            pe.wait_ge(proj_used, 3 * g + 6)

                            def hidden(e):
                                for f in range(2):
                                    if e:
                                        pe.wait_ge(hid_ready, g * 2 * E + 2 * (e - 1) + f + 1)
                                    pe.matmul(bank[:, 1 + f, :], w1[:, e, f * P:(f + 1) * P], XT[:, :],
                                              start=True, stop=True).then_inc(hid_psum, 1)

                            hidden(0)
                            for e in range(E):
                                if e + 1 < E:
                                    hidden(e + 1)
                                pe.wait_ge(hid_ready, g * 2 * E + 2 * e + 2)
                                y_bank(e)
                                for t in range(GT):
                                    for f in range(2):
                                        last = pe.matmul(bank[:, 6 + e % 2, t * P:(t + 1) * P],
                                                         HM[:, e % 2, f, t * P:(t + 1) * P], w2[:, e, f, :],
                                                         start=f == 0, stop=f == 1)
                                last.then_inc(y_psum, 1)

                @block.vector
                def _(dve):
                    dve.sem_inc(x_free, 1)
                    dve.sem_inc(g_ready, 1)
                    dve.sem_inc(proj_used, 3)
                    dve.sem_inc(y_used, 2)
                    dve.sem_inc(qk_stored, 1)
                    dve.sem_inc(v_stored, 1)
                    dve.sem_inc(g_stored, 1)

                    def pick(scores, best, one_hot):
                        dve.tensor_reduce(best, scores, AX.X, ALU.max)
                        dve.drain()
                        dve.tensor_tensor(SEL[:, :, :], scores, best[:, :, None].broadcast_to([P, GT, E]), ALU.is_equal)
                        dve.drain()
                        dve.tensor_tensor(SEL[:, :, :], SEL[:, :, :], rank[:, :, :], ALU.mult)
                        dve.drain()
                        dve.tensor_reduce(MX[:, 2, :], SEL[:, :, :], AX.X, ALU.max)
                        dve.drain()
                        dve.tensor_tensor(one_hot, SEL[:, :, :], MX[:, 2, :, None].broadcast_to([P, GT, E]), ALU.is_equal)
                        dve.drain()

                    with dve.Fori(0, GROUPS) as g:
                        dve.wait_ge(x_in, 16 * g + 16)
                        for t in range(GT):
                            dve.bn_stats(stats[:, t, :], X[:, t, :])
                        dve.drain()
                        for t in range(GT):
                            dve.bn_aggr(mv[:, t, :], stats[:, t, :])
                        dve.drain()
                        dve.tensor_scalar(rstd[:, :], mv[:, :, 1], EPS, None, ALU.add).then_inc(var_ready, 1)
                        dve.wait_ge(rstd_ready, g + 1)
                        for t in range(GT):
                            last = dve.tensor_scalar(XN[:, t, :], X[:, t, :], mv[:, t, 0:1], rstd[:, t:t + 1],
                                                     ALU.subtract, ALU.mult)
                        last.then_inc(xn_ready, 1)
                        dve.drain()
                        dve.sem_inc(x_free, 1)
                        for s in range(streams):
                            dve.wait_ge(proj_psum, 3 * g + min(s, 1) + 1)
                            src = bank[:, 1 + min(s, 1), :]
                            if layer == 0:
                                bias = col[:, 0:1] if s == 0 else bk2[:, s - 1:s]
                                last = dve.tensor_scalar(FQ[:, s, :], src, bias, None, ALU.add)
                            else:
                                last = dve.tensor_scalar(FQ[:, s, :], src, CLAMP, -CLAMP, ALU.min, ALU.max)
                            if s == 0:
                                last.then_inc(proj_used, 1)
                        last.then_inc(proj_used, 1)
                        dve.drain()
                        dve.sem_inc(f_ready, 1)
                        dve.wait_ge(proj_psum, 3 * g + 3)
                        dve.wait_ge(v_stored, 16 * g + 1)
                        vp = bank[:, 3, :].rearrange("p (t h d) -> p t h d", t=GT, d=DH * (1 + layer))
                        if layer == 0:
                            for t in range(GT):
                                last = dve.tensor_tensor(vw[:, t, :, 0:DH], vp[:, t], bv[:, :].rearrange("p (h d) -> p h d", d=DH),
                                                         ALU.add)
                        else:
                            last = dve.tensor_copy(vw[:, :, :, 0:2 * DH], vp)
                        last.then_inc(proj_used, 1)
                        dve.drain()
                        dve.sem_inc(v_ready, 1)
                        dve.wait_ge(p1_ready, g + 1)
                        dve.tensor_tensor(FR[:, 0:streams, :], FQ[:, 0:streams, :], PARTS[:, 0, 0:streams, :],
                                          ALU.subtract).then_inc(r_ready, 1)
                        dve.wait_ge(logits_psum, g + 1)
                        lp = bank[:, 4, 0:GT * E].rearrange("p (t e) -> p t e", e=E)
                        if layer == 0:
                            for t in range(GT):
                                dve.tensor_tensor(LG[:, t, :], lp[:, t], gate_b[:, :], ALU.add)
                        else:
                            dve.tensor_copy(LG[:, :, :], lp)
                        dve.drain()
                        pick(LG[:, :, :], MX[:, 0, :], OH[:, 0, :, :])
                        if layer == 0:
                            dve.tensor_copy(C[:, :, :], OH[:, 0, :, :]).then_inc(c_ready, 1)
                        else:
                            dve.scalar_tensor_tensor(L2[:, :, :], OH[:, 0, :, :], -BIG, LG[:, :, :], ALU.mult, ALU.add)
                            dve.drain()
                            pick(L2[:, :, :], MX[:, 1, :], OH[:, 1, :, :])
                            dve.tensor_tensor(MX[:, 2, :], MX[:, 1, :], MX[:, 0, :], ALU.subtract).then_inc(diff_ready, 1)
                            dve.wait_ge(odds_ready, g + 1)
                            dve.tensor_scalar(MX[:, 0, :], MX[:, 3, :], 1.0, None, ALU.add)
                            dve.drain()
                            dve.reciprocal(MX[:, 1, :], MX[:, 0, :])
                            dve.drain()
                            dve.tensor_tensor(MX[:, 2, :], MX[:, 1, :], MX[:, 3, :], ALU.mult)
                            dve.tensor_tensor(LG[:, :, :], OH[:, 0, :, :], MX[:, 1, :, None].broadcast_to([P, GT, E]), ALU.mult)
                            dve.drain()
                            dve.tensor_tensor(L2[:, :, :], OH[:, 1, :, :], MX[:, 2, :, None].broadcast_to([P, GT, E]), ALU.mult)
                            dve.drain()
                            dve.tensor_tensor(C[:, :, :], LG[:, :, :], L2[:, :, :], ALU.add).then_inc(c_ready, 1)
                        dve.wait_ge(p2_ready, g + 1)
                        dve.tensor_tensor(PARTS[:, 2, 0:streams, :], FR[:, 0:streams, :], PARTS[:, 1, 0:streams, :],
                                          ALU.subtract).then_inc(parts_ready, 1)
                        dve.wait_ge(bias_psum, g + 1)
                        dve.wait_ge(g_ready, g + 1)
                        dve.tensor_copy(ACC[:, :, :], bank[:, 5, :].rearrange("p (t d) -> p t d", t=GT))
                        for e in range(E):
                            dve.drain()
                            dve.wait_ge(y_psum, g * E + e + 1)
                            for t in range(GT):
                                last = dve.scalar_tensor_tensor(ACC[:, t, :], bank[:, 6 + e % 2, t * P:(t + 1) * P],
                                                                C[:, t, e:e + 1], ACC[:, t, :], ALU.mult, ALU.add)
                            last.then_inc(y_used, 1)
                        dve.drain()
                        dve.sem_inc(acc_ready, 1)

        def attention_stage(layer, x_src, dst):
            plan, NMAX, NEXP, NJB = attention_plan(layer)
            n = f"a{layer}_"
            kv_in = sem(n + "kv_in")
            q_in = [sem(n + f"q_in{i}") for i in range(QR)]
            m_in = [sem(n + f"m_in{i}") for i in range(QR)]
            max_psum, max_used = sem(n + "max_psum"), sem(n + "max_used")
            pm_ready = sem(n + "pm_ready")
            m_ready, m_psum, m_split = sem(n + "m_ready"), sem(n + "m_psum"), sem(n + "m_split")
            exp_psum, exp_ready, av_done = sem(n + "exp_psum"), sem(n + "exp_ready"), sem(n + "av_done")
            o_copied, ob_psum, o_normed, ot_psum, ot_ready, s_psum = (
                sem(n + s) for s in ("o_copied", "ob_psum", "o_normed", "ot_psum", "ot_ready", "s_psum"))
            misc_used = sem(n + "misc_used")
            ms_ready, ln_ready, rms_ready = sem(n + "ms_ready"), sem(n + "ln_ready"), sem(n + "rms_ready")
            xg_in = [sem(n + f"xg_in{i}") for i in range(2)]
            final_done = sem(n + "final_done")
            stored = [sem(n + f"stored{i}") for i in range(2)]
            VD = DH * (1 + layer)
            VH = H if layer == 0 else PAIRS
            KVD = 16 * (2 * (2 - layer) + 1)
            QD = 16 * (4 if layer == 0 else 2)
            RING = [len(range(i, NB, QR)) for i in range(QR)]
            x_v = x_src.rearrange("(b i p) d -> b i p d", i=NB, p=P)
            g_v = g_dram.rearrange("(b i p) d -> b i p d", i=NB, p=P)
            d_v = dst.rearrange("(b i p) d -> b i p d", i=NB, p=P)
            v_v = v_dram[layer].rearrange("(b j p) d -> b p j d", j=NB, p=P)
            AV, MISC = 6, 7

            def near(ib, jb):
                return layer == 0 and abs(ib - jb) <= 1

            def side(ib, jb):
                return 1 if layer == 0 and jb > ib + 1 else 0

            def kblock(rows, ib, jb, pair):
                return KS[0:rows, side(ib, jb), pair, jb * P:(jb + 1) * P]

            def near_scores(pe, dst_bank, rows, ib, jb, c):
                q = ib % QR
                view = dst_bank.rearrange("p (h a q) -> p h a q", h=H, a=2)
                for pair in range(PAIRS):
                    qs = QS[0:rows, q, pair, :, :].rearrange("k h (a i) -> k h a i", a=2)[:, :, :, c * CQ:(c + 1) * CQ]
                    pe.matmul(view[:, 2 * pair:2 * pair + 2, :, :], kblock(rows, ib, jb, pair), qs,
                              start=pair == 0, stop=False, skip_group_check=True)
                for i in range(CQ):
                    y = Y0 - ((ib - jb) * P + c * CQ + i)
                    qp = QP[:, q, :, :].rearrange("k h (a i) -> k h a i", a=2)[:, :, :, c * CQ + i]
                    last = pe.matmul(view[:, :, :, i], rel_t[:, y:y + P], qp, start=False, stop=i == CQ - 1,
                                     skip_group_check=True)
                return last

            def far_scores(pe, dst_bank, rows, ib, jb, quad):
                masked = layer == 1 and ib == jb
                for k in range(2):
                    pair = 2 * quad + k
                    last = pe.matmul(dst_bank[:, k * 2 * P:(k + 1) * 2 * P], kblock(rows, ib, jb, pair),
                                     QS[0:rows, ib % QR, pair, :, :].rearrange("k h i -> k (h i)"),
                                     start=k == 0, stop=not masked, skip_group_check=True)
                if masked:
                    last = pe.matmul(dst_bank.rearrange("p (h i) -> p h i", h=4), eye_b[:, :],
                                     mask_b[:, 1:2, :].broadcast_to([P, 4, P]), start=False, stop=True,
                                     skip_group_check=True)
                return last

            with nc.Block() as block:
                @block.sync
                def _(sp):
                    def load_q(b, ib):
                        r = ib % QR
                        sp.wait_ge(o_copied, b * NB + max(ib - QR + 1, 0) + 1)
                        for hh in range(2):
                            src = q_dram[b][:, :, ib * P:(ib + 1) * P].rearrange("(p h) r i -> h r p i", h=2)[hh]
                            sp.dma_start(QS[hh * ROWS:(hh + 1) * ROWS, r, :, hh, :], src).then_inc(q_in[r], 16)
                        if layer == 0:
                            for a in range(2):
                                i0 = ib * P + a * HALF
                                sp.dma_start(QP[a * ROWS:(a + 1) * ROWS, r, :, a * HALF:(a + 1) * HALF],
                                             q_dram[b][:, :, i0:i0 + HALF].rearrange("h r i -> r h i")).then_inc(q_in[r], 16)

                    with sp.Fori(0, B) as b:
                        sp.wait_ge(o_copied, b * NB + 1)
                        load_q(b, 0)
                        for v in range(2 - layer):
                            for hh in range(2):
                                src = k_dram[v][b].rearrange("(p h) r s -> h r p s", h=2)[hh]
                                sp.dma_start(KS[hh * ROWS:(hh + 1) * ROWS, v, :, :], src).then_inc(kv_in, 16)
                        sp.dma_start(VV[:, :, 0:VH * (VD + 1)], v_v[b]).then_inc(kv_in, 16)
                        load_q(b, 1)
                        load_q(b, 2)
                        for it in plan:
                            if it[0] == "msplit":
                                ib = it[1]
                                sp.wait_ge(m_split, b * NB + ib + 1)
                                for k in range(3):
                                    sp.dma_start(QS[KD + k:KD + k + 1, ib % QR, :, :, :].rearrange("o p h i -> o (p h) i"),
                                                 MP[:, ib % 2, k, :]).then_inc(m_in[ib % QR], 16)
                            if it[0] == "oproj" and it[1] + QR < NB:
                                load_q(b, it[1] + QR)
                            if it[0] == "final":
                                ib = it[1]
                                sp.wait_ge(final_done, b * NB + ib + 3)
                                sp.dma_start(d_v[b][ib], XO[:, ib % 2, :]).then_inc(stored[ib % 2], 16)
                    for r in range(2):
                        sp.wait_ge(stored[r], 16 * B * NB // 2 + 1)

                @block.gpsimd
                def _(pool):
                    with pool.Fori(0, B) as b:
                        for ib in range(NB):
                            r = ib % 2
                            pool.wait_ge(final_done, b * NB + ib + 1)
                            pool.sem_inc(waited, 1)
                            pool.dma_start(XG[:, r, 0, :], x_v[b][ib]).then_inc(xg_in[r], 16)
                            pool.dma_start(XG[:, r, 1, :], g_v[b][ib]).then_inc(xg_in[r], 16)

                @block.scalar
                def _(act):
                    with act.Fori(0, B) as b:
                        for it in plan:
                            if it[0] == "exp":
                                _, ib, jb, half, ne, nj = it
                                act.wait_ge(exp_psum, b * NEXP + ne + 1)
                                if half == 0:
                                    act.wait_ge(av_done, b * NJB + nj + 1)
                                k = 2 + 2 * (ne % 2)
                                act.activation(EX[:, nj % ER, half * 1024:(half + 1) * 1024].rearrange("p (c n) -> p c n", c=2),
                                               bank[:, k:k + 2, :], ACT.Exp, scale=SCALE).then_inc(exp_ready, 1)
                            elif it[0] == "ocopy":
                                act.wait_ge(av_done, b * NJB + it[2] + 1 + ER)
                                act.activation(OS[:, :], bank[:, AV, :], ACT.Copy).then_inc(o_copied, 1)
                            elif it[0] == "orms":
                                act.wait_ge(ms_ready, b * NB + it[1] + 1)
                                act.activation(SS[:, :], SS[:, :], ACT.Ln).then_inc(ln_ready, 1)
                                act.wait_ge(ln_ready, b * NB + it[1] + 1)
                                act.activation(SS[:, :], SS[:, :], ACT.Exp, scale=-0.5).then_inc(rms_ready, 1)
                            elif it[0] == "oturned":
                                act.wait_ge(ot_psum, b * NB + it[1] + 1)
                                act.activation(OT[:, :], bank[:, MISC, 0:P], ACT.Copy).then_inc(ot_ready, 1)

                @block.tensor
                def _(pe):
                    with pe.Fori(0, B) as b:
                        misc = [0]

                        def misc_bank():
                            pe.wait_ge(misc_used, b * 3 * NB + misc[0] + 1)
                            misc[0] += 1

                        def operands(ib):
                            pe.wait_ge(q_in[ib % QR], QD * (RING[ib % QR] * b + ib // QR + 1))

                        pe.wait_ge(kv_in, KVD * b + KVD)
                        for it in plan:
                            kind, ib = it[0], it[1]
                            if kind in ("max", "maxt"):
                                nm = it[4]
                                if nm == 0 or seen_ib != ib:
                                    operands(ib)
                                seen_ib = ib
                                pe.wait_ge(max_used, b * NMAX + nm + 1)
                                mb = bank[:, nm % 2, :]
                            if kind == "max" and layer == 0:
                                _, _, jb, c, _ = it
                                if near(ib, jb):
                                    last = near_scores(pe, mb, KD, ib, jb, c)
                                else:
                                    last = far_scores(pe, mb, KD, ib, jb, c)
                                last.then_inc(max_psum, 1)
                            elif kind == "max":
                                _, _, half, h, _ = it
                                j0, j1 = half * 512, min((half + 1) * 512, (ib + 1) * P)
                                diagonal = j1 == (ib + 1) * P
                                last = pe.matmul(mb[:, 0:j1 - j0], QS[0:KD, ib % QR, h // 2, h % 2, :],
                                                 KS[0:KD, 0, h // 2, j0:j1], start=True, stop=not diagonal,
                                                 skip_group_check=True)
                                if diagonal:
                                    last = pe.matmul(mb[:, j1 - j0 - P:j1 - j0], eye_b[:, :], mask_b[:, 0, :],
                                                     start=False, stop=True, skip_group_check=True)
                                last.then_inc(max_psum, 1)
                            elif kind == "maxt":
                                c = it[3]
                                pe.wait_ge(pm_ready, b * NB + ib + 1)
                                for k in range(4):
                                    last = pe.transpose(mb[:, k * P:(k + 1) * P], PM[:, ib % 2, 4 * c + k, :], eye[:, :])
                                last.then_inc(max_psum, 1)
                            elif kind == "mrow":
                                misc_bank()
                                pe.wait_ge(m_ready, b * NB + ib + 1)
                                pe.transpose(bank[0:H, MISC, 0:P], M[:, :], eye[:, :]).then_inc(m_psum, 1)
                            elif kind == "exp":
                                _, _, jb, half, ne, nj = it
                                if jb == 0 and half == 0:
                                    pe.wait_ge(m_in[ib % QR], 48 * (RING[ib % QR] * b + ib // QR + 1))
                                pe.wait_ge(exp_ready, b * NEXP + ne + 1)
                                for k in range(2):
                                    eb = bank[:, 2 + 2 * (ne % 2) + k, :]
                                    if near(ib, jb):
                                        last = near_scores(pe, eb, KM, ib, jb, 2 * half + k)
                                    else:
                                        last = far_scores(pe, eb, KM, ib, jb, 2 * half + k)
                                last.then_inc(exp_psum, 1)
                            elif kind == "av":
                                _, _, jb, nj, njb = it
                                pe.wait_ge(exp_ready, b * NEXP + 2 * nj + 2 + 2)
                                if jb == 0:
                                    pe.wait_ge(o_copied, b * NB + ib + 1)
                                for h in range(H):
                                    r, slot = 32 * (h % 4), h // 4
                                    dst_o = bank[r:r + 32, AV, slot * P:(slot + 1) * P]
                                    vo = (h if layer == 0 else h // 2) * (VD + 1)
                                    ex = EX[:, nj % ER, :]
                                    if near(ib, jb):
                                        ex = ex.rearrange("p (c h a q) -> p h a c q", c=CH, h=H, a=2)[:, h]
                                        dst_o = dst_o.rearrange("p (a c q) -> p a c q", a=2, c=CH)
                                    else:
                                        ex = ex[:, h * P:(h + 1) * P]
                                    last = pe.matmul(dst_o, VV[:, jb, vo:vo + 32], ex, start=jb == 0 and slot == 0,
                                                     stop=jb == njb - 1, skip_group_check=True)
                                last.then_inc(av_done, 1)
                            elif kind == "oback":
                                misc_bank()
                                pe.wait_ge(o_copied, b * NB + ib + 2)
                                for k in range(4):
                                    last = pe.transpose(bank[:, MISC, k * P:(k + 1) * P], OS[:, k * P:(k + 1) * P], eye[:, :])
                                last.then_inc(ob_psum, 1)
                            elif kind == "oturn":
                                misc_bank()
                                pe.wait_ge(o_normed, b * NB + ib + 1)
                                pe.transpose(bank[:, MISC, 0:P], OF[:, :], eye[:, :]).then_inc(ot_psum, 1)
                            elif kind == "oproj":
                                pe.wait_ge(ot_ready, b * NB + ib + 1)
                                last = pe.matmul(bank[:, MISC, P:2 * P], OT[:, :], w["o", layer][:, :],
                                                 start=True, stop=layer == 1)
                                if layer == 0:
                                    last = pe.matmul(bank[:, MISC, P:2 * P], ones_row[:, :], bo[:, :], start=False, stop=True)
                                last.then_inc(s_psum, 1)

                @block.vector
                def _(dve):
                    dve.sem_inc(max_used, 2)
                    dve.sem_inc(exp_ready, 2)
                    dve.sem_inc(av_done, ER)
                    dve.sem_inc(o_copied, 1)
                    dve.sem_inc(misc_used, 1)
                    dve.sem_inc(final_done, 2)
                    dve.sem_inc(stored[0], 1)
                    dve.sem_inc(stored[1], 1)
                    with dve.Fori(0, B) as b:
                        for it in plan:
                            kind, ib = it[0], it[1]
                            if kind in ("max", "maxt"):
                                nm = it[4]
                                mb = bank[:, nm % 2, :]
                            if kind == "max" and layer == 0:
                                _, _, jb, c, _ = it
                                if c == 0:
                                    dve.drain()
                                dve.wait_ge(max_psum, b * NMAX + nm + 1)
                                if near(ib, jb):
                                    pm = PM[:, ib % 2, :, :].rearrange("p h (a c q) -> p h a c q", a=2, c=CH)[:, :, :, c, :]
                                    sc = mb.rearrange("p (h a q) -> p h a q", h=H, a=2)
                                else:
                                    pm = PM[:, ib % 2, 4 * c:4 * c + 4, :].rearrange("p h i -> p (h i)")
                                    sc = mb
                                if jb == 0:
                                    last = dve.tensor_copy(pm, sc)
                                else:
                                    last = dve.tensor_tensor(pm, sc, pm, ALU.max)
                                last.then_inc(max_used, 1)
                                if jb == NB - 1 and c == CH - 1:
                                    dve.drain()
                                    dve.sem_inc(pm_ready, 1)
                            elif kind == "maxt":
                                c = it[3]
                                dve.wait_ge(max_psum, b * NMAX + nm + 1)
                                last = dve.tensor_reduce(M[:, 4 * c:4 * c + 4], mb.rearrange("p (h j) -> p h j", h=4),
                                                         AX.X, ALU.max)
                                last.then_inc(max_used, 1)
                                if c == 3:
                                    dve.drain()
                                    dve.sem_inc(m_ready, 1)
                            elif kind == "max":
                                _, _, half, h, _ = it
                                width = min((half + 1) * 512, (ib + 1) * P) - half * 512
                                dve.wait_ge(max_psum, b * NMAX + nm + 1)
                                two = ib >= 4
                                target = M2[:, h, half:half + 1] if two else M[:, h:h + 1]
                                dve.tensor_reduce(target, mb[:, 0:width], AX.X, ALU.max).then_inc(max_used, 1)
                                if h == H - 1 and half == ib // 4:
                                    dve.drain()
                                    if two:
                                        dve.tensor_tensor(M[:, :], M2[:, :, 0], M2[:, :, 1], ALU.max)
                                        dve.drain()
                                    dve.sem_inc(m_ready, 1)
                            elif kind == "msplit":
                                mp = MP[:, ib % 2, :, :]
                                mt = bank[0:H, MISC, 0:P]
                                dve.wait_ge(m_psum, b * NB + ib + 1)
                                dve.tensor_scalar(mp[:, 0], mt, -1.0, None, ALU.mult)
                                dve.drain()
                                dve.scalar_tensor_tensor(MR[:, :], mt, -1.0, mp[:, 0], ALU.mult, ALU.subtract)\
                                   .then_inc(misc_used, 1)
                                dve.drain()
                                dve.tensor_copy(mp[:, 1], MR[:, :])
                                dve.drain()
                                dve.tensor_tensor(mp[:, 2], MR[:, :], mp[:, 1], ALU.subtract).then_inc(m_split, 1)
                            elif kind == "onorm":
                                o = bank[:, MISC, :].rearrange("p (h d) -> p h d", d=32)
                                dve.wait_ge(ob_psum, b * NB + ib + 1)
                                dve.reciprocal(RC[:, :], o[:, :, VD])
                                dve.drain()
                                if layer == 0:
                                    dve.tensor_tensor(OF[:, :].rearrange("p (h d) -> p h d", d=VD), o[:, :, 0:VD],
                                                      RC[:, :, None].broadcast_to([P, H, VD]), ALU.mult)\
                                       .then_inc(misc_used, 1)
                                    dve.drain()
                                    dve.sem_inc(o_normed, 1)
                                else:
                                    odd = RC[:, :].rearrange("p (a two) -> p a two", two=2)[:, :, 1]
                                    dve.tensor_scalar(odd, odd, neg_lam, None, ALU.mult)
                                    dve.drain()
                                    dve.tensor_tensor(ON[:, :, :], o[:, :, 0:VD], RC[:, :, None].broadcast_to([P, H, VD]),
                                                      ALU.mult).then_inc(misc_used, 1)
                                    dve.drain()
                                    both = ON[:, :, :].rearrange("p (a two) d -> p a two d", two=2)
                                    dve.tensor_tensor(OD[:, :, :], both[:, :, 0, :], both[:, :, 1, :], ALU.add)
                                    dve.drain()
                                    dve.tensor_tensor(OQ[:, :, :], OD[:, :, :], OD[:, :, :], ALU.mult)
                                    dve.drain()
                                    dve.tensor_reduce(SS[:, :], OQ[:, :, :], AX.X, ALU.add)
                                    dve.drain()
                                    dve.tensor_scalar(SS[:, :], SS[:, :], 1.0 / VD, EPS, ALU.mult, ALU.add)\
                                       .then_inc(ms_ready, 1)
                            elif kind == "oscale":
                                dve.wait_ge(rms_ready, b * NB + ib + 1)
                                dve.tensor_scalar(SS[:, :], SS[:, :], 1.0 - LAMBDA_INIT, None, ALU.mult)
                                dve.drain()
                                dve.tensor_tensor(OF[:, :].rearrange("p (h d) -> p h d", d=VD), OD[:, :, :],
                                                  SS[:, :, None].broadcast_to([P, PAIRS, VD]), ALU.mult)\
                                   .then_inc(o_normed, 1)
                            elif kind == "final":
                                r = ib % 2
                                dve.wait_ge(s_psum, b * NB + ib + 1)
                                dve.wait_ge(xg_in[r], 32 * (b * (NB // 2) + ib // 2) + 32)
                                dve.tensor_tensor(TM[:, :], bank[:, MISC, P:2 * P], XG[:, r, 1, :], ALU.mult)\
                                   .then_inc(misc_used, 1)
                                dve.drain()
                                dve.wait_ge(stored[r], 16 * (b * (NB // 2) + ib // 2) + 1)
                                dve.tensor_tensor(XO[:, r, :], TM[:, :], XG[:, r, 0, :], ALU.add).then_inc(final_done, 1)

        xf = ins["x"]
        token_stage(0, xf)
        attention_stage(0, xf, x_mid)
        token_stage(1, x_mid)
        attention_stage(1, x_mid, out)


def kernel(L0_attn_x, L0_attn_Wq, L0_attn_bq, L0_attn_Wk, L0_attn_bk, L0_attn_Wv, L0_attn_bv, L0_attn_Wo, L0_attn_bo,
           L0_attn_rel_table, L0_ffn_gate_w, L0_ffn_gate_b, L0_ffn_expert_w, L0_ffn_expert_b, L1_attn_Wq, L1_attn_Wk,
           L1_attn_Wv, L1_attn_Wo, L1_attn_lq1, L1_attn_lk1, L1_attn_lq2, L1_attn_lk2, L1_ffn_router_w, L1_ffn_w1,
           L1_ffn_b1, L1_ffn_w2, L1_ffn_b2):
    import concourse.bacc as _bacc
    from concourse.bass_utils import run_bass_kernel_spmd as _run

    def rows(a):
        return np.broadcast_to(np.asarray(a)[None], (P,) + np.asarray(a).shape)

    rel = np.asarray(L0_attn_rel_table)
    i = np.arange(P)
    arrays = {
        "x": np.asarray(L0_attn_x).reshape(T, D),
        "eye": np.eye(P, dtype=np.float32),
        "mask": np.stack([np.where(i[None, :] > i[:, None], -BIG, 0.0), np.where(i[:, None] > i[None, :], -BIG, 0.0)], 1)
                  .astype(np.float32),
        "rank": np.broadcast_to((E - np.arange(E)).astype(np.float32), (P, GT, E)),
        "levels": np.tile(np.repeat(np.array([[-(p > 0), -(p > 1)] for p in KPART], np.float32), DH, 0), (2, 1)),
        "rel": position_table_rows(rel),
        "cols": np.stack([np.asarray(L0_attn_bq), np.asarray(L0_attn_bk), np.tile(rel[2 * MAXLEN - 2], H),
                          np.tile(rel[0], H)], 1),
        "bv": rows(L0_attn_bv), "bo": np.asarray(L0_attn_bo)[None], "gate_b": rows(L0_ffn_gate_b),
        "lam": rows(np.stack([np.asarray(a) for a in (L1_attn_lq1, L1_attn_lq2, L1_attn_lk1, L1_attn_lk2)])),
        "gate_w": np.asarray(L0_ffn_gate_w), "router_w": np.asarray(L1_ffn_router_w).T,
        "expert_w": np.asarray(L0_ffn_expert_w).transpose(1, 0, 2), "expert_b": np.asarray(L0_ffn_expert_b),
        "b2": np.asarray(L1_ffn_b2),
        "w1": np.asarray(L1_ffn_w1).transpose(2, 0, 1),
        "b1": np.asarray(L1_ffn_b1).reshape(E, 2, P).transpose(2, 0, 1),
        "w2": np.asarray(L1_ffn_w2).reshape(E, P, 2, P).transpose(3, 0, 2, 1),
        "Wq0": np.asarray(L0_attn_Wq).T, "Wk0": np.asarray(L0_attn_Wk).T,
        "Wv0": np.asarray(L0_attn_Wv).T, "Wo0": np.asarray(L0_attn_Wo).T,
        "Wq1": np.asarray(L1_attn_Wq).T, "Wk1": np.asarray(L1_attn_Wk).T,
        "Wv1": np.asarray(L1_attn_Wv).T, "Wo1": np.asarray(L1_attn_Wo).T,
    }
    nc = _bacc.Bacc("TRN2", target_bir_lowering=False, num_devices=1)
    arrays = {f"in_{k}": np.ascontiguousarray(v) for k, v in arrays.items()}
    ins = {k[3:]: nc.dram_tensor(k, v.shape, mybir.dt.from_np(v.dtype), kind="ExternalInput").ap()
           for k, v in arrays.items()}
    out = nc.dram_tensor("out_dram", (T, D), F32, kind="ExternalOutput").ap()
    build(nc, ins, out)
    r = _run(nc, [arrays], core_ids=[0])
    return r.results[0]["out_dram"].reshape(B, S, D)
```

```python
import concourse.bass as bass
from concourse import mybir
from collections import namedtuple
from contextlib import ExitStack
import numpy as np

F32 = mybir.dt.float32
BF16 = mybir.dt.bfloat16
ALU = mybir.AluOpType
ACT = mybir.ActivationFunctionType
AX = mybir.AxisListType

P = 128
B, S, D = 4, 1024, 128
T = B * S
GROUP = 512
GT = GROUP // P
GROUPS = T // GROUP
H = 16
DH = 8
PAIRS = H // 2
NB = S // P
SLOTS = 6
QPART = [0, 0, 0, 1, 1, 2]
KPART = [0, 1, 2, 0, 1, 0]
ROWS = SLOTS * DH
KD = 2 * ROWS
KM = KD + 3
MAXLEN = 128
CH = 4
HALF = P // 2
CQ = HALF // CH
Y0 = P + HALF - 1
YW = Y0 + 2 * P
E = 8
FF = 256
LAMBDA_INIT = 0.8 - 0.6 * float(np.exp(-0.3 * 6))
EPS = 1e-5
SCALE = float(DH) ** -0.5
BIG = 1e30
TWO_ONES = float(np.array([0x3F803F80], np.uint32).view(np.float32)[0])
CLAMP = 1e18
UNITS = 2 * NB
MR_, XR = 3, 3
ER = 2
QR = 3
AHEAD = 2 * NB


def position_table_rows(rel):
    y = np.arange(YW)
    out = [rel[np.clip(HALF * a + MAXLEN - 1 - (y - Y0), 0, 2 * MAXLEN - 2)].T for a in range(2) for _ in range(SLOTS)]
    return np.concatenate(out, 0)


Step = namedtuple("Step", "kind u jb part n need first last", defaults=(None,) * 6)


def block_order(layer, u):
    k = u % NB
    return k if layer == 0 else (NB - 1 - k // 2 if k % 2 == 0 else k // 2)


def is_near(layer, ib, jb):
    return layer == 0 and abs(ib - jb) <= 1


def attention_plan(layer):
    timed = []

    def spread(begin, end, steps, middle=0.5):
        for k, step in enumerate(steps):
            x = 2 * (k + 0.5) / len(steps)
            timed.append((begin + (end - begin) * (x * middle if x < 1 else middle + (x - 1) * (1 - middle)), step))

    for u in range(UNITS):
        ib = block_order(layer, u)
        keys = NB if layer == 0 else ib + 1
        fars = [jb for jb in range(keys) if not is_near(layer, ib, jb)]
        nears = [jb for jb in range(keys) if is_near(layer, ib, jb)]
        if layer == 0:
            spread(u, u + 0.80, [Step("max", u, jb, c, first=jb == fars[0]) for jb in fars for c in range(CH)])
            spread(u + 0.2, u + 0.80, [Step("near", u, jb, c) for jb in nears for c in range(CH)])
            spread(u + 0.2 + 0.6 / len(nears) + 0.05, u + 0.85,
                   [Step("nmax", u, jb, c, first=jb == nears[1]) for jb in nears[1:] for c in range(CH)])
            spread(u + 0.855, u + 0.865, [Step("merge", u, None, c) for c in range(CH)])
            spread(u + 0.95, u + 0.99, [Step("maxt", u, None, c) for c in range(H // 4)])
            at = {"mrow": 1.02, "msplit": 1.04, "mb": 1.19, "begin": 1.22, "middle": 0.62, "end": 2.16,
                  "ocopy": 2.17, "oback": 2.21, "onorm": 2.25, "oturn": 2.32, "oturned": 2.33, "oproj": 2.38, "final": 2.42}
            spread(u + at["mb"], u + at["mb"] + 0.04, [Step("mb", u, None, c) for c in range(4)])
            spread(u + 1.24, u + 1.5, [Step("nsub", u, jb, c) for jb in nears for c in range(CH)])
        else:
            m = [Step("max", u, 0, (h, 1)) for h in range(H)] if ib >= 4 else []
            heads = max(1, 4 // (ib % 4 + 1))
            m += [Step("max", u, ib // 4, (h, heads)) for h in range(0, H, heads)]
            spread(u, u + 0.92, m)
            at = {"mrow": 1.05, "msplit": 1.1, "begin": 1.35, "end": 2.31, "ocopy": 2.33, "oback": 2.4,
                  "onorm": 2.46, "orms": 2.47, "oturn": 2.9, "oturned": 2.93, "oproj": 2.98, "final": 3.02}
        m, order = [], fars + nears
        for k in range(len(order) + 1):
            for c in range(CH):
                if k < len(order):
                    m.append(Step("nexp" if order[k] in nears else "exp", u, order[k], c))
                if k:
                    m.append(Step("av", u, order[k - 1], c, first=k == 1, last=k == len(order)))
        spread(u + at["begin"], u + at["end"], m, at.get("middle", 0.5))
        timed += [(u + at[kind], Step(kind, u)) for kind in
                  ("mrow", "msplit", "ocopy", "oback", "onorm", "orms", "oturn", "oturned", "oproj", "final") if kind in at]
    raw = [step for _, step in sorted(timed, key=lambda x: x[0])]
    count = {"max": 0, "act": 0, "nsub": 0, "nexp": 0, "far": 0, "av": 0}
    made, plan = {}, []
    for it in raw:
        ring = {"max": "max", "maxt": "max", "near": "act", "mb": "act", "exp": "act", "nsub": "nsub", "nexp": "nexp"}.get(it.kind)
        if ring:
            it = it._replace(n=count[ring])
            count[ring] += 1
            made[it.kind, it.u, it.jb, it.part] = it.n
        if it.kind == "exp":
            if it.part == 0:
                made["far", it.u, it.jb] = count["far"]
                count["far"] += 1
            it = it._replace(need=made["far", it.u, it.jb])
        elif it.kind == "nmax":
            it = it._replace(need=made["near", it.u, it.jb, it.part])
        elif it.kind == "nsub":
            it = it._replace(need=made["mb", it.u, None, 3])
        elif it.kind == "nexp":
            it = it._replace(need=made["nsub", it.u, it.jb, it.part])
        elif it.kind == "av":
            near = is_near(layer, block_order(layer, it.u), it.jb)
            it = it._replace(need=made["nexp", it.u, it.jb, CH - 1] if near else made["exp", it.u, it.jb, it.part],
                             n=None if near else made["far", it.u, it.jb])
        elif it.kind == "ocopy" and layer == 1:
            it = it._replace(need=made["far", it.u, block_order(layer, it.u)])
        plan.append(it)
    return plan, count


def build(nc, ins, out):
    ctx = ExitStack()
    with ctx:
        def sb(name, shape, dt=F32):
            return ctx.enter_context(nc.sbuf_tensor(name, shape, dt))

        def sem(name):
            return ctx.enter_context(nc.semaphore(name))

        def dram(name, shape, dt=F32):
            return nc.dram_tensor(name, shape, dt, kind="Internal").ap()

        bank = ctx.enter_context(nc.psum_tensor("bank", [P, 8, 512], F32))

        eye = sb("eye", [P, P])
        eye_b = sb("eye_b", [P, P], BF16)
        mask_b = sb("mask_b", [P, 2, P], BF16)
        rank = sb("rank", [P, GT, E])
        levels = sb("levels", [KD, 2])
        rel_t = sb("rel_t", [KD, YW], BF16)
        col = sb("col", [P, 5])
        bk2 = sb("bk2", [P, 2])
        bv = sb("bv", [P, D])
        bo = sb("bo", [1, D])
        ones_row = sb("ones_row", [1, P])
        add3 = sb("add3", [KM, P], BF16)
        gate_b = sb("gate_b", [P, E])
        lam_in = sb("lam_in", [P, 4, DH])
        lam_w = sb("lam_w", [P, 2, DH])
        lam_s = sb("lam_s", [P, 4])
        w = {}
        for n in ("q", "k", "v", "o"):
            for layer in range(2):
                w[n, layer] = sb(f"w{n}{layer}", [P, P])
        gate_w = [sb("gate_w0", [P, E]), sb("gate_w1", [P, E])]
        out_b = [sb("out_b0", [E, P]), sb("out_b1", [E, P])]

        KS = sb("KS", [P, 2, 2, PAIRS, S], BF16)
        QS = sb("QS", [P, QR, PAIRS, 2, P], BF16)
        QP = sb("QP", [KD, QR, H, P], BF16)
        VV = sb("VV", [P, 2, NB, 168])
        newton = sb("newton", [P, 8])

        x_mid = dram("x_mid", (T, D))
        g_dram = dram("g_dram", (T, D))
        qk_dram = dram("qk_dram", (3, B, 3, D, S), BF16)
        v_dram = [dram("v_dram0", (T, H * (DH + 1))), dram("v_dram1", (T, PAIRS * (2 * DH + 1)))]

        weights_in = sem("weights_in")
        waited = sem("waited")
        setup_done = sem("setup_done")
        lam_exp = sem("lam_exp")
        lam_sum = sem("lam_sum")

        setup = ctx.enter_context(ExitStack())

        def setup_sb(name, shape, dt=F32):
            return setup.enter_context(nc.sbuf_tensor(name, shape, dt))

        mask_f = setup_sb("mask_f", [P, 2, P])
        rel_f = setup_sb("rel_f", [KD, YW])
        rel_r = setup_sb("rel_r", [KD, YW])
        rel_p = setup_sb("rel_p", [KD, YW], BF16)
        rel_p2 = setup_sb("rel_p2", [KD, YW], BF16)

        loads = [
            (eye[:, :], ins["eye"]), (mask_f[:, :, :], ins["mask"]), (rank[:, :, :], ins["rank"]),
            (levels[:, :], ins["levels"]), (rel_f[:, :], ins["rel"]), (col[:, 0:4], ins["cols"]),
            (bv[:, :], ins["bv"]), (bo[:, :], ins["bo"]), (gate_b[:, :], ins["gate_b"]),
            (lam_in[:, :, :], ins["lam"]), (gate_w[0][:, :], ins["gate_w"]), (gate_w[1][:, :], ins["router_w"]),
            (out_b[0][:, :], ins["expert_b"]), (out_b[1][:, :], ins["b2"]),
        ] + [(w[n, layer][:, :], ins[f"W{n}{layer}"]) for n in "qkvo" for layer in range(2)]
        LOADED = 16 * len(loads)

        with nc.Block() as block:
            @block.sync
            def _(sp):
                for dst, src in loads:
                    sp.dma_start(dst, src).then_inc(weights_in, 16)

            @block.gpsimd
            def _(pool):
                pool.memset(QS[:, :, :, :, :].bitcast(F32), 0.0)
                pool.memset(QP[:, :, :, :].bitcast(F32), 0.0)
                pool.memset(KS[:, 1, :, :, :].bitcast(F32), TWO_ONES)
                pool.memset(ones_row[:, :], 1.0)
                pool.memset(add3[0:KD, :], 0.0)
                pool.drain()
                pool.memset(add3[KD:KM, :], 1.0)
                pool.drain()
                pool.memset(VV[:, :, :, :], 0.0).then_inc(setup_done, 1)
                pool.drain()

            @block.vector
            def _(dve):
                dve.memset(KS[:, 0, :, :, :].bitcast(F32), TWO_ONES)
                dve.wait_ge(weights_in, LOADED)
                dve.tensor_copy(eye_b[:, :], eye[:, :])
                dve.tensor_copy(mask_b[:, :, :], mask_f[:, :, :])
                dve.tensor_scalar(bk2[:, 0:1], col[:, 1:2], col[:, 2:3], None, ALU.add)
                dve.tensor_scalar(bk2[:, 1:2], col[:, 1:2], col[:, 3:4], None, ALU.add)
                dve.tensor_scalar(rel_r[:, :], rel_f[:, :], rel_f[:, 0:1], None, ALU.subtract)
                dve.drain()
                dve.tensor_copy(rel_p[:, :], rel_r[:, :])
                dve.drain()
                dve.scalar_tensor_tensor(rel_f[:, :], rel_p[:, :], levels[:, 0:1], rel_r[:, :], ALU.mult, ALU.add)
                dve.drain()
                dve.tensor_copy(rel_p2[:, :], rel_f[:, :])
                dve.drain()
                dve.scalar_tensor_tensor(rel_t[:, :], rel_p2[:, :], levels[:, 1:2], rel_f[:, :], ALU.mult, ALU.add)
                dve.tensor_tensor(lam_w[:, :, :], lam_in[:, 0:2, :], lam_in[:, 2:4, :], ALU.mult)
                dve.drain()
                dve.tensor_reduce(lam_s[:, 0:2], lam_w[:, :, :], AX.X, ALU.add).then_inc(lam_sum, 1)
                dve.wait_ge(lam_exp, 1)
                dve.tensor_tensor(lam_s[:, 2:3], lam_s[:, 1:2], lam_s[:, 0:1], ALU.subtract)
                dve.drain()
                dve.tensor_scalar(lam_s[:, 3:4], lam_s[:, 2:3], -LAMBDA_INIT, None, ALU.add).then_inc(setup_done, 1)

            @block.scalar
            def _(act):
                act.wait_ge(lam_sum, 1)
                act.activation(lam_s[:, 0:2], lam_s[:, 0:2], ACT.Exp).then_inc(lam_exp, 1)

        setup.close()
        neg_lam = lam_s[:, 3:4]

        def rsqrt(eng, y, v, t, fused):
            i32 = mybir.dt.int32
            eng.tensor_scalar(y.bitcast(i32), v.bitcast(i32), -0.5, float(0x5F3759DF), ALU.mult, ALU.add)
            for _ in range(3):
                eng.drain()
                if fused:
                    eng.scalar_tensor_tensor(t, y, -0.5, y, ALU.mult, ALU.mult)
                    eng.drain()
                    eng.tensor_tensor(t, t, v, ALU.mult)
                    eng.drain()
                    eng.scalar_tensor_tensor(y, t, 1.5, y, ALU.add, ALU.mult)
                else:
                    eng.tensor_tensor(t, y, y, ALU.mult)
                    eng.drain()
                    eng.tensor_tensor(t, t, v, ALU.mult)
                    eng.drain()
                    eng.tensor_scalar(t, t, -0.5, 1.5, ALU.mult, ALU.add)
                    eng.drain()
                    eng.tensor_tensor(y, y, t, ALU.mult)
            eng.drain()

        def token_stage(layer, x_src, stage):
            n = f"t{layer}_"
            streams = 3 if layer == 0 else 2
            HV, VD = (H, DH) if layer == 0 else (PAIRS, 2 * DH)
            v_ones = sem(n + "v_ones")

            def local(name, shape, dt=F32):
                return stage.enter_context(nc.sbuf_tensor(f"{n}{name}", shape, dt))

            X = local("X", [P, GT, P])
            stats = local("stats", [P, GT, 6])
            mv = local("mv", [P, GT, 2])
            var = local("var", [P, GT])
            rstd = local("rstd", [P, GT])
            XN = local("XN", [P, GT, P])
            XT = local("XT", [P, 2, GROUP])
            FQ = local("FQ", [P, 3, GROUP])
            FR = local("FR", [P, 3, GROUP])
            PARTS = local("PARTS", [P, 3, 3, GROUP], BF16)
            VA = local("VA", [P, GT, HV, VD + 1])
            LG = local("LG", [P, GT, E])
            L2 = local("L2", [P, GT, E])
            SEL = local("SEL", [P, GT, E])
            OH = local("OH", [P, 2, GT, E])
            MX = local("MX", [P, 4, GT])
            C = local("C", [P, 2, GT, E])
            lean = local("lean", [P, GT])
            CT = local("CT", [E, GROUP])
            HM = local("HM", [P, 2, 2, GROUP])
            ACC = local("ACC", [P, 2, GT, P])
            GE = local("GE", [P, GT, P])
            HA = local("HA", [P, GT, P])
            G = local("G", [P, GT, P])

            x_in, x_free = sem(n + "x_in"), sem(n + "x_free")
            xn_ready, xt_psum, xt_ready = sem(n + "xn_ready"), sem(n + "xt_psum"), sem(n + "xt_ready")
            proj_psum, proj_used = sem(n + "proj_psum"), sem(n + "proj_used")
            f_ready, p1_ready, r_ready, p2_ready = (sem(n + s) for s in ("f_ready", "p1_ready", "r_ready", "p2_ready"))
            parts_ready, v_ready, qk_stored, v_stored = (sem(n + s) for s in ("parts_ready", "v_ready", "qk_stored", "v_stored"))
            logits_psum, c_ready, ct_psum, ct_ready, bias_psum, bias_used = (
                sem(n + s) for s in ("logits_psum", "c_ready", "ct_psum", "ct_ready", "bias_psum", "bias_used"))
            diff_ready, lean_ready = sem(n + "diff_ready"), sem(n + "lean_ready")
            hid_psum, hid_ready = sem(n + "hid_psum"), sem(n + "hid_ready")
            y_psum, y_used = sem(n + "y_psum"), sem(n + "y_used")
            acc_ready, ge_ready, g_ready, g_stored = (sem(n + s) for s in ("acc_ready", "ge_ready", "g_ready", "g_stored"))
            expert_in = sem(n + "expert_in")
            if layer == 0:
                exp_w = local("exp_w", [P, E, P])
                expert_loads = [(exp_w[:, :, :], ins["expert_w"])]
            else:
                w1 = local("w1", [P, E, FF])
                b1 = local("b1", [P, E, 2])
                w2 = local("w2", [P, E, 2, P])
                expert_loads = [(w1[:, :, :], ins["w1"]), (b1[:, :, :], ins["b1"]), (w2[:, :, :, :], ins["w2"])]
            SMALL, QB, KB, VB, HB, YB = 0, 1, 2, 3, 4, 6
            x_v = x_src.rearrange("(g t p) d -> g p t d", t=GT, p=P)
            g_v = g_dram.rearrange("(g t p) d -> g p t d", t=GT, p=P)
            v_v = v_dram[layer].rearrange("(g t p) d -> g p t d", t=GT, p=P)

            def steps(body, g, p, experts=True, front=True, gate=True):
                for e in range(E):
                    if experts:
                        body("expert", g, p, e)
                    if e == 4 and gate:
                        body("gate", g - 1, 1 - p, None)
                    if front:
                        body("front", g + 1, 1 - p, e)

            def run(eng, body):
                steps(body, -1, 1, experts=False, gate=False)
                steps(body, 0, 0, gate=False)
                with eng.Fori(0, GROUPS // 2 - 1) as pair:
                    steps(body, 2 * pair + 1, 1)
                    steps(body, 2 * pair + 2, 0)
                steps(body, GROUPS - 1, 1, front=False)
                body("gate", GROUPS - 1, 1, None)

            with nc.Block() as block:
                @block.gpsimd
                def _(pool):
                    pool.dma_start(X[:, :, :], x_v[0]).then_inc(x_in, 16)
                    pool.memset(VA[:, :, :, VD:VD + 1], 1.0).then_inc(v_ones, 1)

                    def parts(f):
                        pool.wait_ge(p1_ready, f + 1)
                        pool.tensor_tensor(FR[:, 0:streams, :], FQ[:, 0:streams, :], PARTS[:, 0, 0:streams, :],
                                           ALU.subtract).then_inc(r_ready, 1)
                        pool.wait_ge(p2_ready, f + 1)
                        pool.tensor_tensor(PARTS[:, 2, 0:streams, :], FR[:, 0:streams, :], PARTS[:, 1, 0:streams, :],
                                           ALU.subtract).then_inc(parts_ready, 1)

                    with pool.Fori(0, GROUPS - 1) as f:
                        pool.wait_ge(x_free, f + 1)
                        pool.sem_inc(waited, 1)
                        pool.dma_start(X[:, :, :], x_v[f + 1]).then_inc(x_in, 16)
                        parts(f)
                    parts(GROUPS - 1)

                @block.sync
                def _(sp):
                    def store_v(f):
                        sp.wait_ge(v_ready, f + 1)
                        sp.dma_start(v_v[f], VA[:, :, :, :].rearrange("p t h d -> p t (h d)")).then_inc(v_stored, 16)

                    def store_qk(b, c):
                        f, span = 2 * b + c, slice(c * GROUP, (c + 1) * GROUP)
                        sp.wait_ge(parts_ready, f + 1)
                        for s in range(streams):
                            sp.dma_start(qk_dram[s][b][:, :, span].rearrange("r f s -> f r s"), PARTS[:, :, s, :]).then_inc(qk_stored, 16)

                    def store_gate(f):
                        sp.wait_ge(g_ready, f + 1)
                        sp.dma_start(g_v[f], G[:, :, :]).then_inc(g_stored, 16)

                    for to, src in expert_loads:
                        sp.dma_start(to, src).then_inc(expert_in, 16)
                    sp.wait_ge(v_ones, 1)
                    for c in range(2):
                        store_v(c)
                        store_qk(0, c)
                    with sp.Fori(1, B) as b:
                        for c in range(2):
                            store_v(2 * b + c)
                            store_gate(2 * b + c - 2)
                            store_qk(b, c)
                    store_gate(GROUPS - 2)
                    store_gate(GROUPS - 1)
                    sp.wait_ge(v_stored, 16 * GROUPS + 1)
                    sp.wait_ge(qk_stored, 16 * streams * GROUPS + 1)
                    sp.wait_ge(g_stored, 16 * GROUPS + 1)

                @block.scalar
                def _(act):
                    if layer == 0:
                        act.wait_ge(setup_done, 2)

                    def body(kind, f, p, k):
                        if kind == "expert" and layer == 1:
                            if k == 0 and type(f) is int and f == 0:
                                act.wait_ge(expert_in, 16 * len(expert_loads))
                            for h in range(2):
                                act.wait_ge(hid_psum, f * 2 * E + 2 * k + h + 1)
                                act.activation(HM[:, k % 2, h, :], bank[:, HB + h, :], ACT.Gelu,
                                               bias=b1[:, k, h:h + 1]).then_inc(hid_ready, 1)
                        if kind == "gate":
                            act.wait_ge(acc_ready, f + 1)
                            if layer == 0:
                                act.wait_ge(g_stored, 16 * f + 1)
                                act.activation(G[:, :, :], ACC[:, p, :, :], ACT.Silu).then_inc(g_ready, 1)
                            else:
                                act.activation(GE[:, :, :], ACC[:, p, :, :], ACT.Tanh, scale=0.5)
                                act.activation(HA[:, :, :], ACC[:, p, :, :], ACT.Copy, scale=0.5).then_inc(ge_ready, 1)
                        if kind == "front" and k == 1:
                            act.wait_ge(xt_psum, f + 1)
                            act.activation(XT[:, p, :], bank[:, SMALL, :], ACT.Copy).then_inc(xt_ready, 1)
                        if kind == "front" and k == 2 and layer == 0:
                            for st in range(streams):
                                act.wait_ge(proj_psum, 3 * f + min(st, 1) + 1)
                                bias = col[:, 0:1] if st == 0 else bk2[:, st - 1:st]
                                last = act.activation(FQ[:, st, :], bank[:, QB + min(st, 1), :], ACT.Identity, bias=bias)
                                if st == 0:
                                    last.then_inc(proj_used, 1)
                            last.then_inc(proj_used, 1)
                            act.drain()
                            act.sem_inc(f_ready, 1)
                        if kind == "front" and k == 3:
                            act.wait_ge(qk_stored, f * 16 * streams + 1)
                            act.wait_ge(f_ready, f + 1)
                            act.activation(PARTS[:, 0, 0:streams, :], FQ[:, 0:streams, :], ACT.Copy).then_inc(p1_ready, 1)
                        if kind == "front" and k == 4 and layer == 1:
                            act.wait_ge(diff_ready, f + 1)
                            act.activation(lean[:, :], MX[:, 2, :], ACT.Tanh, scale=0.5).then_inc(lean_ready, 1)
                        if kind == "front" and k == 6:
                            act.wait_ge(ct_psum, f + 1)
                            act.activation(CT[:, :], bank[0:E, SMALL, :], ACT.Copy).then_inc(ct_ready, 1)
                        if kind == "front" and k == 7:
                            act.wait_ge(r_ready, f + 1)
                            act.activation(PARTS[:, 1, 0:streams, :], FR[:, 0:streams, :], ACT.Copy).then_inc(p2_ready, 1)
                            act.wait_ge(bias_psum, f + 1)
                            act.activation(ACC[:, p, :, :].rearrange("p t d -> p (t d)"), bank[:, SMALL, :], ACT.Copy)\
                               .then_inc(bias_used, 1)

                    run(act, body)

                @block.tensor
                def _(pe):
                    if layer == 0:
                        pe.wait_ge(weights_in, LOADED)
                        pe.wait_ge(setup_done, 2)

                    def tile(p, t):
                        return XT[:, p, t * P:(t + 1) * P]

                    def hidden(g, p, e):
                        for h in range(2):
                            pe.wait_ge(hid_ready, g * 2 * E + 2 * e + h + 1)
                            pe.matmul(bank[:, HB + h, :], w1[:, e, h * P:(h + 1) * P], XT[:, p, :],
                                      start=True, stop=True).then_inc(hid_psum, 1)

                    def body(kind, f, p, k):
                        if kind == "expert":
                            if k == 0 and type(f) is int and f == 0:
                                pe.wait_ge(expert_in, 16 * len(expert_loads))
                            if layer == 1:
                                if k == 0 and type(f) is int and f == 0:
                                    hidden(0, 0, 0)
                                if k + 1 < E:
                                    hidden(f, p, k + 1)
                                elif not (type(f) is int and f == GROUPS - 1):
                                    hidden(f + 1, 1 - p, 0)
                                pe.wait_ge(hid_ready, f * 2 * E + 2 * k + 2 + 2)
                            pe.wait_ge(y_used, f * E + k + 1)
                            for t in range(GT):
                                y = bank[:, YB + k % 2, t * P:(t + 1) * P]
                                if layer == 0:
                                    last = pe.matmul(y, tile(p, t), exp_w[:, k, :], start=True, stop=True)
                                else:
                                    for h in range(2):
                                        last = pe.matmul(y, HM[:, k % 2, h, t * P:(t + 1) * P], w2[:, k, h, :],
                                                         start=h == 0, stop=h == 1)
                            last.then_inc(y_psum, 1)
                        if kind == "front" and k == 1:
                            pe.wait_ge(bias_used, f + 1)
                            pe.wait_ge(xn_ready, f + 1)
                            for t in range(GT):
                                last = pe.transpose(bank[:, SMALL, t * P:(t + 1) * P], XN[:, t, :], eye[:, :])
                            last.then_inc(xt_psum, 1)
                        if kind == "front" and k == 2:
                            pe.wait_ge(xt_ready, f + 1)
                            pe.wait_ge(proj_used, 3 * f + 3)
                            pe.matmul(bank[:, QB, :], w["q", layer][:, :], XT[:, p, :], start=True, stop=True)\
                              .then_inc(proj_psum, 1)
                            pe.matmul(bank[:, KB, :], w["k", layer][:, :], XT[:, p, :], start=True, stop=True)\
                              .then_inc(proj_psum, 1)
                            for t in range(GT):
                                last = pe.matmul(bank[:, VB, t * P:(t + 1) * P], tile(p, t), w["v", layer][:, :],
                                                 start=True, stop=True)
                            last.then_inc(proj_psum, 1)
                            for t in range(GT):
                                last = pe.matmul(bank[:, SMALL, t * E:(t + 1) * E], tile(p, t), gate_w[layer][:, :],
                                                 start=True, stop=True)
                            last.then_inc(logits_psum, 1)
                        if kind == "front" and k == 6:
                            pe.wait_ge(c_ready, f + 1)
                            for t in range(GT):
                                last = pe.transpose(bank[0:E, SMALL, t * P:(t + 1) * P], C[:, p, t, :], eye[:, :])
                            last.then_inc(ct_psum, 1)
                        if kind == "front" and k == 7:
                            pe.wait_ge(ct_ready, f + 1)
                            for t in range(GT):
                                last = pe.matmul(bank[:, SMALL, t * P:(t + 1) * P], CT[:, t * P:(t + 1) * P],
                                                 out_b[layer][:, :], start=True, stop=True)
                            last.then_inc(bias_psum, 1)

                    run(pe, body)

                @block.vector
                def _(dve):
                    dve.sem_inc(bias_used, 1)
                    dve.sem_inc(proj_used, 3)
                    dve.sem_inc(y_used, 2)
                    dve.sem_inc(hid_ready, 2)
                    dve.sem_inc(qk_stored, 1)
                    dve.sem_inc(v_stored, 1)
                    dve.sem_inc(g_stored, 1)

                    def spread(a):
                        return a[:, :, None].broadcast_to([P, GT, E])

                    def pick(scores, best, one_hot):
                        dve.tensor_reduce(best, scores, AX.X, ALU.max)
                        dve.drain()
                        dve.tensor_tensor(SEL[:, :, :], scores, spread(best), ALU.is_equal)
                        dve.drain()
                        dve.tensor_tensor(SEL[:, :, :], SEL[:, :, :], rank[:, :, :], ALU.mult)
                        dve.drain()
                        dve.tensor_reduce(MX[:, 3, :], SEL[:, :, :], AX.X, ALU.max)
                        dve.drain()
                        dve.tensor_tensor(one_hot, SEL[:, :, :], spread(MX[:, 3, :]), ALU.is_equal)
                        dve.drain()

                    def normalise(f):
                        dve.wait_ge(x_in, 16 * f + 16)
                        for t in range(GT):
                            dve.bn_stats(stats[:, t, :], X[:, t, :])
                        dve.drain()
                        for t in range(GT):
                            dve.bn_aggr(mv[:, t, :], stats[:, t, :])
                        dve.drain()
                        dve.tensor_scalar(var[:, :], mv[:, :, 1], EPS, None, ALU.add)
                        dve.drain()
                        rsqrt(dve, rstd[:, :], var[:, :], newton[:, 0:GT], fused=True)
                        for t in range(GT):
                            last = dve.tensor_scalar(XN[:, t, :], X[:, t, :], mv[:, t, 0:1], rstd[:, t:t + 1],
                                                     ALU.subtract, ALU.mult)
                        last.then_inc(xn_ready, 1)
                        dve.drain()
                        dve.sem_inc(x_free, 1)

                    def take_projections(f):
                        if layer == 1:
                            for s in range(streams):
                                dve.wait_ge(proj_psum, 3 * f + s + 1)
                                dve.tensor_scalar(FQ[:, s, :], bank[:, QB + s, :], CLAMP, -CLAMP, ALU.min, ALU.max)\
                                   .then_inc(proj_used, 1)
                            dve.drain()
                            dve.sem_inc(f_ready, 1)
                        dve.wait_ge(proj_psum, 3 * f + 3)
                        dve.wait_ge(v_stored, 16 * f + 1)
                        vp = bank[:, VB, :].rearrange("p (t h d) -> p t h d", t=GT, d=DH * (1 + layer))
                        if layer == 0:
                            for t in range(GT):
                                last = dve.tensor_tensor(VA[:, t, :, 0:DH], vp[:, t],
                                                         bv[:, :].rearrange("p (h d) -> p h d", d=DH), ALU.add)
                        else:
                            last = dve.tensor_copy(VA[:, :, :, 0:2 * DH], vp)
                        last.then_inc(proj_used, 1)
                        dve.drain()
                        dve.sem_inc(v_ready, 1)

                    def route(f, p):
                        dve.wait_ge(logits_psum, f + 1)
                        lp = bank[:, SMALL, 0:GT * E].rearrange("p (t e) -> p t e", e=E)
                        if layer == 0:
                            for t in range(GT):
                                dve.tensor_tensor(LG[:, t, :], lp[:, t], gate_b[:, :], ALU.add)
                        else:
                            dve.tensor_copy(LG[:, :, :], lp)
                        dve.drain()
                        pick(LG[:, :, :], MX[:, 0, :], OH[:, 0, :, :])
                        if layer == 0:
                            dve.tensor_copy(C[:, p, :, :], OH[:, 0, :, :]).then_inc(c_ready, 1)
                        else:
                            dve.scalar_tensor_tensor(L2[:, :, :], OH[:, 0, :, :], -BIG, LG[:, :, :], ALU.mult, ALU.add)
                            dve.drain()
                            pick(L2[:, :, :], MX[:, 1, :], OH[:, 1, :, :])
                            dve.tensor_tensor(MX[:, 2, :], MX[:, 1, :], MX[:, 0, :], ALU.subtract).then_inc(diff_ready, 1)

                    def router_weights(f, p):
                        dve.wait_ge(lean_ready, f + 1)
                        dve.tensor_scalar(MX[:, 1, :], lean[:, :], -0.5, 0.5, ALU.mult, ALU.add)
                        dve.tensor_scalar(MX[:, 2, :], lean[:, :], 0.5, 0.5, ALU.mult, ALU.add)
                        dve.drain()
                        dve.tensor_tensor(LG[:, :, :], OH[:, 0, :, :], spread(MX[:, 1, :]), ALU.mult)
                        dve.tensor_tensor(L2[:, :, :], OH[:, 1, :, :], spread(MX[:, 2, :]), ALU.mult)
                        dve.drain()
                        dve.tensor_tensor(C[:, p, :, :], LG[:, :, :], L2[:, :, :], ALU.add).then_inc(c_ready, 1)

                    def body(kind, f, p, k):
                        if kind == "expert":
                            dve.drain()
                            if k == 0:
                                dve.wait_ge(bias_used, f + 2)
                            dve.wait_ge(y_psum, f * E + k + 1)
                            for t in range(GT):
                                last = dve.scalar_tensor_tensor(ACC[:, p, t, :], bank[:, YB + k % 2, t * P:(t + 1) * P],
                                                                C[:, p, t, k:k + 1], ACC[:, p, t, :], ALU.mult, ALU.add)
                            last.then_inc(y_used, 1)
                            if k == E - 1:
                                dve.drain()
                                dve.sem_inc(acc_ready, 1)
                        if kind == "gate" and layer == 1:
                            dve.wait_ge(ge_ready, f + 1)
                            dve.wait_ge(g_stored, 16 * f + 1)
                            dve.scalar_tensor_tensor(G[:, :, :], GE[:, :, :], 1.0, HA[:, :, :], ALU.add, ALU.mult)\
                               .then_inc(g_ready, 1)
                        if kind == "front" and k == 0:
                            normalise(f)
                        if kind == "front" and k == 2:
                            take_projections(f)
                        if kind == "front" and k == 3:
                            route(f, p)
                        if kind == "front" and k == 4 and layer == 1:
                            router_weights(f, p)

                    run(dve, body)

        def attention_stage(layer, x_src, dst, stage):
            plan, count = attention_plan(layer)
            NMAX, NACT, NFAR, NSUB, NNEXP = (count[k] for k in ("max", "act", "far", "nsub", "nexp"))
            n = f"a{layer}_"

            def local(name, shape, dt=F32):
                return stage.enter_context(nc.sbuf_tensor(f"{n}{name}", shape, dt))

            EX = local("EX", [P, ER, H * P])
            SN = local("SN", [P, 2, 3, CH, 512])
            MB = local("MB", [P, H, P])
            PN = local("PN", [P, CH, 512])
            PM = local("PM", [P, H, P])
            M2 = local("M2", [P, H, 2])
            M = local("M", [P, 2, H])
            MP = local("MP", [H, 2, 3, P], BF16)
            MR = local("MR", [H, P])
            OS = local("OS", [P, 512])
            RC = local("RC", [P, H])
            ON = local("ON", [P, H, 2 * DH])
            OD = local("OD", [P, PAIRS, 2 * DH])
            OQ = local("OQ", [P, PAIRS, 2 * DH])
            SS = local("SS", [P, PAIRS])
            RS = local("RS", [P, PAIRS])
            rms_tmp = local("rms_tmp", [P, PAIRS])
            OF = local("OF", [P, P])
            OT = local("OT", [P, P])
            XG = local("XG", [P, 2, 2, P])
            TM = local("TM", [P, P])
            XO = local("XO", [P, 2, P])

            kv_in = [sem(n + f"kv_in{i}") for i in range(2)]
            q_in = [sem(n + f"q_in{i}") for i in range(QR)]
            m_in = [sem(n + f"m_in{i}") for i in range(QR)]
            max_psum, max_used = sem(n + "max_psum"), sem(n + "max_used")
            pm_ready = sem(n + "pm_ready")
            m_ready, m_psum, m_split = sem(n + "m_ready"), sem(n + "m_psum"), sem(n + "m_split")
            act_psum, act_done, av_done = sem(n + "act_psum"), sem(n + "act_done"), sem(n + "av_done")
            nsub_done, nexp_done, av_last = sem(n + "nsub_done"), sem(n + "nexp_done"), sem(n + "av_last")
            o_copied, ob_psum, o_normed, ot_psum, ot_ready, s_psum = (
                sem(n + s) for s in ("o_copied", "ob_psum", "o_normed", "ot_psum", "ot_ready", "s_psum"))
            misc_used = sem(n + "misc_used")
            on_ready = sem(n + "on_ready")
            xg_in = [sem(n + f"xg_in{i}") for i in range(2)]
            final_done = sem(n + "final_done")
            stored = [sem(n + f"stored{i}") for i in range(2)]
            VD = DH * (1 + layer)
            VH = H if layer == 0 else PAIRS
            KVD = 16 * (2 * SLOTS * (2 - layer) + 1)
            QRUNS = [(0, 3, 0), (3, 2, 1), (5, 1, 2)]
            QD = 16 * SLOTS * (4 if layer == 0 else 2)
            RING = [len(range(i, UNITS, QR)) for i in range(QR)]
            PAIRS_OF_BATCHES = B // 2
            x_v = x_src.rearrange("(c u p) d -> c u p d", u=UNITS, p=P)
            g_v = g_dram.rearrange("(c u p) d -> c u p d", u=UNITS, p=P)
            d_v = dst.rearrange("(c u p) d -> c u p d", u=UNITS, p=P)
            v_v = v_dram[layer].rearrange("(c b j p) d -> c b p j d", b=2, j=NB, p=P)
            qk_v = qk_dram.rearrange("s (c b) r (h d) i -> s c b r h d i", b=2, d=DH)
            SB, AV, MISC = MR_, 6, 7

            def ring_wait(eng, count, per_pair, c, k, ring, before):
                eng.wait_ge(count, c * per_pair + max(k - ring + 1, 0) + before)

            def block_of(u):
                return block_order(layer, u)

            def near(u, jb):
                return is_near(layer, block_of(u), jb)

            def near_buffer(u, jb):
                return SN[:, u % 2, jb - block_of(u) + 1, :, :]

            def chunk_of(a, part):
                return a.rearrange("p h (a c q) -> p h a c q", a=2, c=CH)[:, :, :, part, :]

            def as_near(a):
                return a.rearrange("p (h a q) -> p h a q", h=H, a=2)

            def kblock(rows, u, jb, pair):
                side = 1 if layer == 0 and jb > block_of(u) + 1 else 0
                return KS[0:rows, u // NB, side, pair, jb * P:(jb + 1) * P]

            def near_scores(pe, dst_bank, rows, u, jb, c):
                q = u % QR
                view = dst_bank.rearrange("p (h a q) -> p h a q", h=H, a=2)
                for pair in range(PAIRS):
                    qs = QS[0:rows, q, pair, :, :].rearrange("k h (a i) -> k h a i", a=2)[:, :, :, c * CQ:(c + 1) * CQ]
                    pe.matmul(view[:, 2 * pair:2 * pair + 2, :, :], kblock(rows, u, jb, pair), qs,
                              start=pair == 0, stop=False, skip_group_check=True)
                for i in range(CQ):
                    y = Y0 - ((block_of(u) - jb) * P + c * CQ + i)
                    qp = QP[:, q, :, :].rearrange("k h (a i) -> k h a i", a=2)[:, :, :, c * CQ + i]
                    last = pe.matmul(view[:, :, :, i], rel_t[:, y:y + P], qp, start=False, stop=i == CQ - 1,
                                     skip_group_check=True)
                return last

            def far_scores(pe, dst_bank, rows, u, jb, quad):
                masked = layer == 1 and block_of(u) == jb
                for k in range(2):
                    pair = 2 * quad + k
                    last = pe.matmul(dst_bank[:, k * 2 * P:(k + 1) * 2 * P], kblock(rows, u, jb, pair),
                                     QS[0:rows, u % QR, pair, :, :].rearrange("k h i -> k (h i)"),
                                     start=k == 0, stop=not masked, skip_group_check=True)
                if masked:
                    last = pe.matmul(dst_bank.rearrange("p (h i) -> p h i", h=4), eye_b[:, :],
                                     mask_b[:, 1:2, :].broadcast_to([P, 4, P]), start=False, stop=True,
                                     skip_group_check=True)
                return last

            with nc.Block() as block:
                @block.sync
                def _(sp):
                    def load_q(c, u):
                        r, i0 = u % QR, block_of(u) * P
                        for s0, ns, part in QRUNS:
                            src = qk_v[0, c, u // NB, part].rearrange("(p h) d i -> h d p i", h=2)
                            for s in range(s0, s0 + ns):
                                for hh in range(2):
                                    row = hh * ROWS + s * DH
                                    sp.dma_start(QS[row:row + DH, r, :, hh, :], src[hh][:, :, i0:i0 + P]).then_inc(q_in[r], 16)
                                if layer == 0:
                                    for a in range(2):
                                        row = a * ROWS + s * DH
                                        i1 = i0 + a * HALF
                                        sp.dma_start(QP[row:row + DH, r, :, a * HALF:(a + 1) * HALF],
                                                     qk_v[0, c, u // NB, part].rearrange("h d i -> d h i")[:, :, i1:i1 + HALF])\
                                          .then_inc(q_in[r], 16)

                    def load_kv(c, lb):
                        for v in range(2 - layer):
                            for s in range(SLOTS):
                                for hh in range(2):
                                    row = hh * ROWS + s * DH
                                    src = qk_v[1 + v, c, lb, KPART[s]].rearrange("(p h) d i -> h d p i", h=2)[hh]
                                    sp.dma_start(KS[row:row + DH, lb, v, :, :], src).then_inc(kv_in[lb], 16)
                        sp.dma_start(VV[:, lb, :, 0:VH * (VD + 1)], v_v[c][lb]).then_inc(kv_in[lb], 16)

                    load_q(0, 0)
                    load_kv(0, 0)
                    load_q(0, 1)
                    load_q(0, 2)
                    load_kv(0, 1)
                    for c, it in ((c, it) for c in range(PAIRS_OF_BATCHES) for it in plan):
                        u = it.u
                        if it.kind == "msplit":
                            sp.wait_ge(m_split, c * UNITS + u + 1)
                            for k in range(3):
                                sp.dma_start(QS[KD + k:KD + k + 1, u % QR, :, :, :].rearrange("o p h i -> o (p h) i"),
                                             MP[:, u % 2, k, :]).then_inc(m_in[u % QR], 16)
                        if it.kind == "ocopy":
                            sp.wait_ge(o_copied, c * UNITS + u + 1 + AHEAD)
                            if u + QR < UNITS:
                                load_q(c, u + QR)
                            elif c + 1 < PAIRS_OF_BATCHES:
                                load_q(c + 1, u % QR)
                            if u % NB == NB - 1 and c + 1 < PAIRS_OF_BATCHES:
                                load_kv(c + 1, u // NB)
                        if it.kind == "final":
                            sp.wait_ge(final_done, c * UNITS + u + 1 + 2)
                            sp.dma_start(d_v[c][u // NB * NB + block_of(u)], XO[:, u % 2, :]).then_inc(stored[u % 2], 16)
                    for r in range(2):
                        sp.wait_ge(stored[r], 16 * B * NB // 2 + 1)

                @block.gpsimd
                def _(pool):
                    def load_xg(c, u):
                        r, row = u % 2, u // NB * NB + block_of(u)
                        pool.wait_ge(final_done, c * UNITS + u + 1)
                        pool.sem_inc(waited, 1)
                        pool.dma_start(XG[:, r, 0, :], x_v[c][row]).then_inc(xg_in[r], 16)
                        pool.dma_start(XG[:, r, 1, :], g_v[c][row]).then_inc(xg_in[r], 16)

                    with pool.Fori(0, PAIRS_OF_BATCHES) as c:
                        load_xg(c, 0)
                        load_xg(c, 1)
                        for it in plan:
                            if it.kind == "nsub":
                                pool.wait_ge(act_done, c * NACT + it.need + 1 + XR)
                                sn = as_near(near_buffer(it.u, it.jb)[:, it.part, :])
                                pool.tensor_tensor(sn, sn, chunk_of(MB[:, :, :], it.part), ALU.add).then_inc(nsub_done, 1)
                            elif it.kind == "orms":
                                pool.wait_ge(on_ready, c * UNITS + it.u + 1)
                                both = ON[:, :, :].rearrange("p (a two) d -> p a two d", two=2)
                                pool.tensor_tensor(OD[:, :, :], both[:, :, 0, :], both[:, :, 1, :], ALU.add)
                                pool.drain()
                                pool.tensor_tensor(OQ[:, :, :], OD[:, :, :], OD[:, :, :], ALU.mult)
                                pool.drain()
                                for width in (8, 4, 2):
                                    pool.tensor_tensor(OQ[:, :, 0:width], OQ[:, :, 0:width], OQ[:, :, width:2 * width], ALU.add)
                                    pool.drain()
                                pool.tensor_tensor(SS[:, :], OQ[:, :, 0], OQ[:, :, 1], ALU.add)
                                pool.drain()
                                pool.tensor_scalar(SS[:, :], SS[:, :], 1.0 / VD, EPS, ALU.mult, ALU.add)
                                pool.drain()
                                rsqrt(pool, RS[:, :], SS[:, :], rms_tmp[:, :], fused=False)
                                pool.tensor_scalar(RS[:, :], RS[:, :], 1.0 - LAMBDA_INIT, None, ALU.mult)
                                pool.drain()
                                pool.tensor_tensor(OF[:, :].rearrange("p (h d) -> p h d", d=VD), OD[:, :, :],
                                                  RS[:, :, None].broadcast_to([P, PAIRS, VD]), ALU.mult)\
                                   .then_inc(o_normed, 1)
                            elif it.kind == "final" and it.u + 2 < UNITS:
                                load_xg(c, it.u + 2)

                @block.scalar
                def _(act):
                    with act.Fori(0, PAIRS_OF_BATCHES) as c:
                        for it in plan:
                            kind, u, jb, part = it.kind, it.u, it.jb, it.part
                            if kind in ("near", "mb", "exp"):
                                act.wait_ge(act_psum, c * NACT + it.n + 1)
                                src = bank[:, SB + it.n % XR, :]
                            if kind == "near":
                                act.activation(near_buffer(u, jb)[:, part, :], src, ACT.Copy).then_inc(act_done, 1)
                            elif kind == "mb":
                                act.activation(MB[:, 4 * part:4 * part + 4, :].rearrange("p h i -> p (h i)"), src, ACT.Copy)\
                                   .then_inc(act_done, 1)
                            elif kind == "exp":
                                if part == 0:
                                    ring_wait(act, av_done, NFAR, c, it.need, ER, ER)
                                act.activation(EX[:, it.need % ER, part * 512:(part + 1) * 512], src, ACT.Exp, scale=SCALE)\
                                   .then_inc(act_done, 1)
                            elif kind == "nexp":
                                act.wait_ge(nsub_done, c * NSUB + it.need + 1)
                                sn = near_buffer(u, jb)[:, part, :]
                                act.activation(sn, sn, ACT.Exp, scale=SCALE).then_inc(nexp_done, 1)
                            elif kind == "ocopy":
                                if layer == 0:
                                    act.wait_ge(av_last, c * UNITS + u + 1)
                                else:
                                    act.wait_ge(av_done, c * NFAR + it.need + 1 + ER)
                                act.activation(OS[:, :], bank[:, AV, :], ACT.Copy).then_inc(o_copied, 1)
                            elif kind == "oturned":
                                act.wait_ge(ot_psum, c * UNITS + u + 1)
                                act.activation(OT[:, :], bank[:, MISC, 0:P], ACT.Copy).then_inc(ot_ready, 1)

                @block.tensor
                def _(pe):
                    with pe.Fori(0, PAIRS_OF_BATCHES) as c:
                        misc = [0]
                        seen = None

                        def misc_bank():
                            pe.wait_ge(misc_used, c * 3 * UNITS + misc[0] + 1)
                            misc[0] += 1

                        for it in plan:
                            kind, u, jb, part = it.kind, it.u, it.jb, it.part
                            r = u % QR
                            if kind in ("max", "near") and seen != u:
                                seen = u
                                pe.wait_ge(q_in[r], QD * (RING[r] * c + u // QR + 1))
                                if u % NB == 0:
                                    pe.wait_ge(kv_in[u // NB], KVD * (c + 1))
                            if kind in ("max", "maxt"):
                                ring_wait(pe, max_used, NMAX, c, it.n, MR_, MR_)
                                mb = bank[:, it.n % MR_, :]
                            if kind in ("near", "mb", "exp"):
                                ring_wait(pe, act_done, NACT, c, it.n, XR, XR)
                                eb = bank[:, SB + it.n % XR, :]
                            if kind == "max" and layer == 0:
                                far_scores(pe, mb, KD, u, jb, part).then_inc(max_psum, 1)
                            elif kind == "near":
                                near_scores(pe, eb, KD, u, jb, part).then_inc(act_psum, 1)
                            elif kind == "max":
                                h0, heads = part
                                j0, j1 = jb * 512, min((jb + 1) * 512, (block_of(u) + 1) * P)
                                width, diagonal = j1 - j0, j1 == (block_of(u) + 1) * P
                                for k in range(heads):
                                    h = h0 + k
                                    last = pe.matmul(mb[:, k * width:(k + 1) * width], QS[0:KD, r, h // 2, h % 2, :],
                                                     KS[0:KD, u // NB, 0, h // 2, j0:j1], start=k == 0,
                                                     stop=not diagonal, skip_group_check=True)
                                if diagonal:
                                    out_m = mb[:, 0:heads * width].rearrange("p (h j) -> p h j", h=heads)
                                    last = pe.matmul(out_m[:, :, width - P:width], eye_b[:, :],
                                                     mask_b[:, 0:1, :].broadcast_to([P, heads, P]),
                                                     start=False, stop=True, skip_group_check=True)
                                last.then_inc(max_psum, 1)
                            elif kind == "maxt":
                                pe.wait_ge(pm_ready, c * UNITS + u + 1)
                                for k in range(4):
                                    last = pe.transpose(mb[:, k * P:(k + 1) * P], PM[:, 4 * part + k, :], eye[:, :])
                                last.then_inc(max_psum, 1)
                            elif kind == "mrow":
                                misc_bank()
                                pe.wait_ge(m_ready, c * UNITS + u + 1)
                                pe.transpose(bank[0:H, MISC, 0:P], M[:, u % 2, :], eye[:, :]).then_inc(m_psum, 1)
                            elif kind == "mb":
                                if part == 0:
                                    pe.wait_ge(m_in[r], 48 * (RING[r] * c + u // QR + 1))
                                for k in range(2):
                                    last = pe.matmul(eb[:, k * 2 * P:(k + 1) * 2 * P], add3[:, :],
                                                     QS[0:KM, r, 2 * part + k, :, :].rearrange("k h i -> k (h i)"),
                                                     start=True, stop=True)
                                last.then_inc(act_psum, 1)
                            elif kind == "exp":
                                if layer == 1 and jb == 0 and part == 0:
                                    pe.wait_ge(m_in[r], 48 * (RING[r] * c + u // QR + 1))
                                far_scores(pe, eb, KM, u, jb, part).then_inc(act_psum, 1)
                            elif kind == "av":
                                if near(u, jb):
                                    if part == 0:
                                        pe.wait_ge(nexp_done, c * NNEXP + it.need + 1)
                                else:
                                    pe.wait_ge(act_done, c * NACT + it.need + 1 + XR)
                                if it.first and part == 0:
                                    pe.wait_ge(o_copied, c * UNITS + u + AHEAD)
                                for k in range(4):
                                    h = 4 * part + k
                                    dst_o = bank[32 * k:32 * k + 32, AV, part * P:(part + 1) * P]
                                    vo = (h if layer == 0 else h // 2) * (VD + 1)
                                    if near(u, jb):
                                        ex = near_buffer(u, jb).rearrange("p c (h a q) -> p h a c q", h=H, a=2)[:, h]
                                        dst_o = dst_o.rearrange("p (a c q) -> p a c q", a=2, c=CH)
                                    else:
                                        ex = EX[:, it.n % ER, h * P:(h + 1) * P]
                                    last = pe.matmul(dst_o, VV[:, u // NB, jb, vo:vo + 32], ex,
                                                     start=bool(it.first) and part == 0, stop=bool(it.last),
                                                     skip_group_check=True)
                                if part == CH - 1 and not near(u, jb):
                                    last.then_inc(av_done, 1)
                                elif part == CH - 1 and it.last:
                                    last.then_inc(av_last, 1)
                            elif kind == "oback":
                                misc_bank()
                                pe.wait_ge(o_copied, c * UNITS + u + 1 + AHEAD)
                                for k in range(4):
                                    last = pe.transpose(bank[:, MISC, k * P:(k + 1) * P], OS[:, k * P:(k + 1) * P], eye[:, :])
                                last.then_inc(ob_psum, 1)
                            elif kind == "oturn":
                                misc_bank()
                                pe.wait_ge(o_normed, c * UNITS + u + 1)
                                pe.transpose(bank[:, MISC, 0:P], OF[:, :], eye[:, :]).then_inc(ot_psum, 1)
                            elif kind == "oproj":
                                pe.wait_ge(ot_ready, c * UNITS + u + 1)
                                last = pe.matmul(bank[:, MISC, P:2 * P], OT[:, :], w["o", layer][:, :],
                                                 start=True, stop=layer == 1)
                                if layer == 0:
                                    last = pe.matmul(bank[:, MISC, P:2 * P], ones_row[:, :], bo[:, :], start=False, stop=True)
                                last.then_inc(s_psum, 1)

                @block.vector
                def _(dve):
                    dve.sem_inc(max_used, MR_)
                    dve.sem_inc(act_done, XR)
                    dve.sem_inc(av_done, ER)
                    dve.sem_inc(o_copied, AHEAD)
                    dve.sem_inc(misc_used, 1)
                    dve.sem_inc(final_done, 2)
                    dve.sem_inc(stored[0], 1)
                    dve.sem_inc(stored[1], 1)
                    with dve.Fori(0, PAIRS_OF_BATCHES) as c:
                        for it in plan:
                            kind, u, jb, part = it.kind, it.u, it.jb, it.part
                            if kind in ("max", "maxt"):
                                dve.wait_ge(max_psum, c * NMAX + it.n + 1)
                                mb = bank[:, it.n % MR_, :]
                            if kind == "max" and layer == 0:
                                pm = PM[:, 4 * part:4 * part + 4, :].rearrange("p h i -> p (h i)")
                                if it.first:
                                    dve.tensor_copy(pm, mb).then_inc(max_used, 1)
                                else:
                                    dve.tensor_tensor(pm, mb, pm, ALU.max).then_inc(max_used, 1)
                                if part == CH - 1:
                                    dve.drain()
                            elif kind == "nmax":
                                dve.wait_ge(act_done, c * NACT + it.need + 1 + XR)
                                before = near_buffer(u, jb - 1)[:, part, :] if it.first else PN[:, part, :]
                                dve.tensor_tensor(PN[:, part, :], near_buffer(u, jb)[:, part, :], before, ALU.max)
                                if part == CH - 1:
                                    dve.drain()
                            elif kind == "merge":
                                pm = chunk_of(PM[:, :, :], part)
                                dve.tensor_tensor(pm, as_near(PN[:, part, :]), pm, ALU.max)
                                if part == CH - 1:
                                    dve.drain()
                                    dve.sem_inc(pm_ready, 1)
                            elif kind == "maxt":
                                dve.tensor_reduce(M[:, u % 2, 4 * part:4 * part + 4], mb.rearrange("p (h j) -> p h j", h=4),
                                                  AX.X, ALU.max).then_inc(max_used, 1)
                                if part == 3:
                                    dve.drain()
                                    dve.sem_inc(m_ready, 1)
                            elif kind == "max":
                                (h0, heads), ib = part, block_of(u)
                                width = min((jb + 1) * 512, (ib + 1) * P) - jb * 512
                                two = ib >= 4
                                target = M2[:, h0:h0 + heads, jb] if two else M[:, u % 2, h0:h0 + heads]
                                dve.tensor_reduce(target, mb[:, 0:heads * width].rearrange("p (h j) -> p h j", h=heads),
                                                  AX.X, ALU.max).then_inc(max_used, 1)
                                if h0 + heads == H and jb == ib // 4:
                                    dve.drain()
                                    if two:
                                        dve.tensor_tensor(M[:, u % 2, :], M2[:, :, 0], M2[:, :, 1], ALU.max)
                                        dve.drain()
                                    dve.sem_inc(m_ready, 1)
                            elif kind == "msplit":
                                mp = MP[:, u % 2, :, :]
                                mt = bank[0:H, MISC, 0:P]
                                dve.wait_ge(m_psum, c * UNITS + u + 1)
                                dve.tensor_scalar(mp[:, 0], mt, -1.0, None, ALU.mult)
                                dve.drain()
                                dve.scalar_tensor_tensor(MR[:, :], mt, -1.0, mp[:, 0], ALU.mult, ALU.subtract)\
                                   .then_inc(misc_used, 1)
                                dve.drain()
                                dve.tensor_copy(mp[:, 1], MR[:, :])
                                dve.drain()
                                dve.tensor_tensor(mp[:, 2], MR[:, :], mp[:, 1], ALU.subtract).then_inc(m_split, 1)
                            elif kind == "onorm":
                                o = bank[:, MISC, :].rearrange("p (h d) -> p h d", d=32)
                                dve.wait_ge(ob_psum, c * UNITS + u + 1)
                                dve.reciprocal(RC[:, :], o[:, :, VD])
                                dve.drain()
                                if layer == 0:
                                    dve.tensor_tensor(OF[:, :].rearrange("p (h d) -> p h d", d=VD), o[:, :, 0:VD],
                                                      RC[:, :, None].broadcast_to([P, H, VD]), ALU.mult)\
                                       .then_inc(misc_used, 1)
                                    dve.drain()
                                    dve.sem_inc(o_normed, 1)
                                else:
                                    odd = RC[:, :].rearrange("p (a two) -> p a two", two=2)[:, :, 1]
                                    dve.tensor_scalar(odd, odd, neg_lam, None, ALU.mult)
                                    dve.drain()
                                    dve.tensor_tensor(ON[:, :, :], o[:, :, 0:VD], RC[:, :, None].broadcast_to([P, H, VD]),
                                                      ALU.mult).then_inc(misc_used, 1)
                                    dve.drain()
                                    dve.sem_inc(on_ready, 1)
                            elif kind == "final":
                                r = u % 2
                                dve.wait_ge(s_psum, c * UNITS + u + 1)
                                dve.wait_ge(xg_in[r], 32 * (c * NB + u // 2) + 32)
                                dve.tensor_tensor(TM[:, :], bank[:, MISC, P:2 * P], XG[:, r, 1, :], ALU.mult)\
                                   .then_inc(misc_used, 1)
                                dve.drain()
                                dve.wait_ge(stored[r], 16 * (c * NB + u // 2) + 1)
                                dve.tensor_tensor(XO[:, r, :], TM[:, :], XG[:, r, 0, :], ALU.add).then_inc(final_done, 1)

        xf = ins["x"]
        for layer, (src, dst) in enumerate(((xf, x_mid), (x_mid, out))):
            with ExitStack() as stage:
                token_stage(layer, src, stage)
            with ExitStack() as stage:
                attention_stage(layer, src, dst, stage)


def kernel(L0_attn_x, L0_attn_Wq, L0_attn_bq, L0_attn_Wk, L0_attn_bk, L0_attn_Wv, L0_attn_bv, L0_attn_Wo, L0_attn_bo,
           L0_attn_rel_table, L0_ffn_gate_w, L0_ffn_gate_b, L0_ffn_expert_w, L0_ffn_expert_b, L1_attn_Wq, L1_attn_Wk,
           L1_attn_Wv, L1_attn_Wo, L1_attn_lq1, L1_attn_lk1, L1_attn_lq2, L1_attn_lk2, L1_ffn_router_w, L1_ffn_w1,
           L1_ffn_b1, L1_ffn_w2, L1_ffn_b2):
    import concourse.bacc as _bacc
    from concourse.bass_utils import run_bass_kernel_spmd as _run

    def rows(a):
        return np.broadcast_to(np.asarray(a)[None], (P,) + np.asarray(a).shape)

    rel = np.asarray(L0_attn_rel_table)
    i = np.arange(P)
    arrays = {
        "x": np.asarray(L0_attn_x).reshape(T, D),
        "eye": np.eye(P, dtype=np.float32),
        "mask": np.stack([np.where(i[None, :] > i[:, None], -BIG, 0.0), np.where(i[:, None] > i[None, :], -BIG, 0.0)], 1)
                  .astype(np.float32),
        "rank": np.broadcast_to((E - np.arange(E)).astype(np.float32), (P, GT, E)),
        "levels": np.tile(np.repeat(np.array([[-(p > 0), -(p > 1)] for p in KPART], np.float32), DH, 0), (2, 1)),
        "rel": position_table_rows(rel),
        "cols": np.stack([np.asarray(L0_attn_bq), np.asarray(L0_attn_bk), np.tile(rel[2 * MAXLEN - 2], H),
                          np.tile(rel[0], H)], 1),
        "bv": rows(L0_attn_bv), "bo": np.asarray(L0_attn_bo)[None], "gate_b": rows(L0_ffn_gate_b),
        "lam": rows(np.stack([np.asarray(a) for a in (L1_attn_lq1, L1_attn_lq2, L1_attn_lk1, L1_attn_lk2)])),
        "gate_w": np.asarray(L0_ffn_gate_w), "router_w": np.asarray(L1_ffn_router_w).T,
        "expert_w": np.asarray(L0_ffn_expert_w).transpose(1, 0, 2), "expert_b": np.asarray(L0_ffn_expert_b),
        "b2": np.asarray(L1_ffn_b2),
        "w1": np.asarray(L1_ffn_w1).transpose(2, 0, 1),
        "b1": np.asarray(L1_ffn_b1).reshape(E, 2, P).transpose(2, 0, 1),
        "w2": np.asarray(L1_ffn_w2).reshape(E, P, 2, P).transpose(3, 0, 2, 1),
        "Wq0": np.asarray(L0_attn_Wq).T, "Wk0": np.asarray(L0_attn_Wk).T,
        "Wv0": np.asarray(L0_attn_Wv).T, "Wo0": np.asarray(L0_attn_Wo).T,
        "Wq1": np.asarray(L1_attn_Wq).T, "Wk1": np.asarray(L1_attn_Wk).T,
        "Wv1": np.asarray(L1_attn_Wv).T, "Wo1": np.asarray(L1_attn_Wo).T,
    }
    nc = _bacc.Bacc("TRN2", target_bir_lowering=False, num_devices=1)
    arrays = {f"in_{k}": np.ascontiguousarray(v) for k, v in arrays.items()}
    ins = {k[3:]: nc.dram_tensor(k, v.shape, mybir.dt.from_np(v.dtype), kind="ExternalInput").ap()
           for k, v in arrays.items()}
    out = nc.dram_tensor("out_dram", (T, D), F32, kind="ExternalOutput").ap()
    build(nc, ins, out)
    r = _run(nc, [arrays], core_ids=[0])
    return r.results[0]["out_dram"].reshape(B, S, D)
```
